# Optimizing a Trainium2 kernel written in Bass

```python
import numpy as np
import jax
import jax.numpy as jnp

def _softmax(x, axis=-1):
    return jax.nn.softmax(x, axis=axis)

def _gelu(x):
    return jax.nn.gelu(x, approximate=True)

def _silu(x):
    return jax.nn.silu(x)

def _sigmoid(x):
    return jax.nn.sigmoid(x)

def _layernorm(x, axis=-1, eps=1e-05):
    m = jnp.mean(x, axis=axis, keepdims=True)
    v = jnp.var(x, axis=axis, keepdims=True)
    return (x - m) / jnp.sqrt(v + eps)

def _scatter_add(tgt, idx, src, axis=0):
    return tgt.at[idx].add(src)

def _segment_sum(src, seg, n):
    return jax.ops.segment_sum(src, seg, n)
kernel_name = 'mk_gnn_ffn_d1_gnn_r32_88c1e4'

def setup_inputs(seed: int=0):
    np.random.seed(seed)
    _w = jnp.asarray

    def _rec_inputs():
        import jax
        import jax.numpy as jnp
        _gk = jax.random.key(seed)
        x = -0.0002117 + 1 * jax.random.normal(jax.random.fold_in(_gk, 1), (3125, 256), jnp.float32)
        _s = jax.random.randint(jax.random.fold_in(_gk, 2), (25000,), 0, 3125, jnp.int32)
        _d = jax.random.randint(jax.random.fold_in(_gk, 3), (25000,), 0, 3125, jnp.int32)
        _loop = jnp.arange(3125, dtype=jnp.int32)
        src = jnp.concatenate([_s, _d, _loop])
        dst = jnp.concatenate([_d, _s, _loop])
        _o = jnp.argsort(dst, stable=True)
        src = src[_o]
        dst = dst[_o]
        return (x, src, dst)
    x, src, dst = _rec_inputs()

    def _L0_gnn_setup():
        import jax, jax.numpy as jnp
        import numpy as np
        N_NODES = 3125
        N_EDGES = 100000
        IN_CH = 256
        OUT_CH = 256
        key = jax.random.key(seed)
        k1, k2, k3, k4, k5 = jax.random.split(key, 5)
        x = jax.random.normal(k1, (N_NODES, IN_CH), dtype=jnp.float32)
        src = jax.random.randint(k2, (N_EDGES,), 0, N_NODES, dtype=jnp.int64)
        dst = jax.random.randint(k3, (N_EDGES,), 0, N_NODES, dtype=jnp.int64)
        bound = 1.0 / np.sqrt(IN_CH)
        weight = jax.random.uniform(k4, (IN_CH, OUT_CH), minval=-bound, maxval=bound, dtype=jnp.float32)
        bias = jax.random.uniform(k5, (OUT_CH,), minval=-bound, maxval=bound, dtype=jnp.float32)
        return {'x': x, 'src': src, 'dst': dst, 'weight': weight, 'bias': bias}
    _L0_gnn_all = _L0_gnn_setup()
    _L0_gnn_in = {k: v for k, v in _L0_gnn_all.items() if k in ('weight', 'bias')}
    del _L0_gnn_all

    def _L0_ffn_setup():
        import jax, jax.numpy as jnp
        import numpy as np
        from jax import lax
        key = jax.random.key(seed)
        B, T, I, H = (64, 64, 256, 256)
        ks = jax.random.split(key, 13)
        s = 1.0 / np.sqrt(H)

        def w(k, shape):
            return jax.random.uniform(k, shape, jnp.float32, -s, s)
        return {'x': jax.random.normal(ks[0], (B, T, I), jnp.float32), 'U_i': w(ks[1], (I, H)), 'V_i': w(ks[2], (H, H)), 'b_i': w(ks[3], (H,)), 'U_f': w(ks[4], (I, H)), 'V_f': w(ks[5], (H, H)), 'b_f': w(ks[6], (H,)), 'U_c': w(ks[7], (I, H)), 'V_c': w(ks[8], (H, H)), 'b_c': w(ks[9], (H,)), 'U_o': w(ks[10], (I, H)), 'V_o': w(ks[11], (H, H)), 'b_o': w(ks[12], (H,))}
    _L0_ffn_all = _L0_ffn_setup()
    _L0_ffn_in = {k: v for k, v in _L0_ffn_all.items() if k in ('U_i', 'V_i', 'b_i', 'U_f', 'V_f', 'b_f', 'U_c', 'V_c', 'b_c', 'U_o', 'V_o', 'b_o')}
    del _L0_ffn_all
    return {'x': x, 'src': src, 'dst': dst, 'L0_gnn_weight': _L0_gnn_in['weight'], 'L0_gnn_bias': _L0_gnn_in['bias'], 'L0_ffn_U_i': _L0_ffn_in['U_i'], 'L0_ffn_V_i': _L0_ffn_in['V_i'], 'L0_ffn_b_i': _L0_ffn_in['b_i'], 'L0_ffn_U_f': _L0_ffn_in['U_f'], 'L0_ffn_V_f': _L0_ffn_in['V_f'], 'L0_ffn_b_f': _L0_ffn_in['b_f'], 'L0_ffn_U_c': _L0_ffn_in['U_c'], 'L0_ffn_V_c': _L0_ffn_in['V_c'], 'L0_ffn_b_c': _L0_ffn_in['b_c'], 'L0_ffn_U_o': _L0_ffn_in['U_o'], 'L0_ffn_V_o': _L0_ffn_in['V_o'], 'L0_ffn_b_o': _L0_ffn_in['b_o']}

def reference(x, src, dst, L0_gnn_weight, L0_gnn_bias, L0_ffn_U_i, L0_ffn_V_i, L0_ffn_b_i, L0_ffn_U_f, L0_ffn_V_f, L0_ffn_b_f, L0_ffn_U_c, L0_ffn_V_c, L0_ffn_b_c, L0_ffn_U_o, L0_ffn_V_o, L0_ffn_b_o):
    import jax
    import jax.numpy as jnp

    def _L0_gnn_ref(x, src, dst, weight, bias):
        import jax, jax.numpy as jnp
        import numpy as np
        N_NODES = 3125
        N_EDGES = 100000
        IN_CH = 256
        OUT_CH = 256
        h = jnp.matmul(x, weight) + bias
        agg = jax.ops.segment_sum(h[src], dst, num_segments=N_NODES)
        deg = jax.ops.segment_sum(jnp.ones((src.shape[0],), dtype=h.dtype), dst, num_segments=N_NODES)
        deg = jnp.maximum(deg, 1.0)[:, None]
        return agg / deg

    def _L0_ffn_ref(x, U_i, V_i, b_i, U_f, V_f, b_f, U_c, V_c, b_c, U_o, V_o, b_o):
        import jax, jax.numpy as jnp
        import numpy as np
        from jax import lax
        B, T, _ = x.shape
        H = U_i.shape[1]
        xt = jnp.swapaxes(x, 0, 1)
        xi = xt @ U_i + b_i
        xf = xt @ U_f + b_f
        xg = xt @ U_c + b_c
        xo = xt @ U_o + b_o
        h0 = jnp.zeros((B, H), x.dtype)
        c0 = jnp.zeros((B, H), x.dtype)

        def step(carry, xs):
            h, c = carry
            xi_t, xf_t, xg_t, xo_t = xs
            i_t = jax.nn.sigmoid(xi_t + h @ V_i)
            f_t = jax.nn.sigmoid(xf_t + h @ V_f)
            g_t = jnp.tanh(xg_t + h @ V_c)
            o_t = jax.nn.sigmoid(xo_t + h @ V_o)
            c_new = h * c + i_t * g_t
            h_new = o_t * jnp.tanh(c_new)
            return ((h_new, c_new), h_new)
        (_, _), hs = lax.scan(step, (h0, c0), (xi, xf, xg, xo))
        return jnp.swapaxes(hs, 0, 1)
    x = x + _L0_gnn_ref(_layernorm(x, axis=-1), src, dst, L0_gnn_weight, L0_gnn_bias)
    x = x + _L0_ffn_ref(_layernorm(x, axis=-1)[None], L0_ffn_U_i, L0_ffn_V_i, L0_ffn_b_i, L0_ffn_U_f, L0_ffn_V_f, L0_ffn_b_f, L0_ffn_U_c, L0_ffn_V_c, L0_ffn_b_c, L0_ffn_U_o, L0_ffn_V_o, L0_ffn_b_o)[0]
    return x

_drawn_inputs = setup_inputs


def setup_inputs(seed=0):
    import zlib

    import numpy as np

    out = dict(_drawn_inputs(seed))
    spreads = {}
    factors = {'L0_ffn_V_i': 8.0,
     'L0_ffn_b_i': 22.853,
     'L0_ffn_V_c': 3.851,
     'L0_ffn_b_c': 7.032,
     'L0_ffn_V_o': 8.0,
     'L0_ffn_b_o': 8.0}
    for name, (base, spread) in spreads.items():
        noise = np.random.default_rng([zlib.crc32(name.encode()), seed]).standard_normal(out[name].shape)
        drawn = base * np.exp(spread * noise) if base else spread * noise
        out[name] = jnp.asarray(drawn.astype(out[name].dtype))
    for name, factor in factors.items():
        out[name] = (out[name] * factor).astype(out[name].dtype)
    return out
```

```python
from contextlib import ExitStack

import concourse.bass as bass
from concourse import mybir

F32 = mybir.dt.float32
I32 = mybir.dt.int32
U32 = mybir.dt.uint32
ALU = mybir.AluOpType
ACT = mybir.ActivationFunctionType
AX_X = mybir.AxisListType.X

P = 128
EPS = 1e-5

GROUP_TILES = 4
WIN = 64

STEPS = 25
WARM_FROM = 5
STATE_TOL = 2.0 ** -18


def bass_gnn_lstm_kernel(nc, x, src, dst, w_gnn, b_gnn, U_i, V_i, b_i, U_c, V_c, b_c, U_o, V_o, b_o, out):
    N, D = x.shape
    E = src.shape[0]
    H = U_i.shape[1]
    DH = D // P
    HH = H // P
    CHUNKS = N // STEPS
    GROUP = GROUP_TILES * P
    GROUPS = -(-E // GROUP)
    TAIL = E - (GROUPS - 1) * GROUP
    TAIL_P, TAIL_J = divmod(TAIL, GROUP_TILES)
    PASSES = -(-N // WIN)
    PAIRS = GROUPS // 2
    MT = 3 * HH
    BLOCK = 4
    COLS = [(0, (CHUNKS + 1) // 2), ((CHUNKS + 1) // 2, CHUNKS)]
    assert N == CHUNKS * STEPS and D == DH * P and H == HH * P and D == H and CHUNKS <= P and GROUPS <= P and GROUPS % 2 == 0

    z_dram = nc.dram_tensor("z_dram", (N, D), F32, kind="Internal").ap()
    win_dram = nc.dram_tensor("win_dram", (GROUPS, 2), F32, kind="Internal").ap()

    with ExitStack() as ctx:
        def sb(name, shape, dt=F32):
            return ctx.enter_context(nc.sbuf_tensor(name, shape, dt))

        def ps(name, shape, dt=F32):
            return ctx.enter_context(nc.psum_tensor(name, shape, dt))

        def sem(name):
            return ctx.enter_context(nc.semaphore(name))

        x_sb = sb("x_sb", [CHUNKS, STEPS, D])
        gx = sb("gx", [P, STEPS, MT, CHUNKS])
        z_sb = gx[0:CHUNKS, :, :, :].rearrange("p s m k -> p (s m k)")[:, 0:STEPS * D].rearrange(
            "p (s d) -> p s d", s=STEPS)
        agg = sb("agg", [P, DH + 1, N + WIN])
        SLOT = HH * CHUNKS
        h_all = agg[:, :, :].rearrange("p a n -> p (a n)")[:, 0:(STEPS + 1) * SLOT].rearrange(
            "p (s m k) -> p s m k", s=STEPS + 1, m=HH)
        c_all = sb("c_all", [P, STEPS + 1, HH, CHUNKS])
        c_flat = c_all[:, :, :, :].rearrange("p s m k -> p (s m k)")
        Z2T = 2 * DH * BLOCK * CHUNKS
        z2T = c_flat[:, 0:Z2T].rearrange("p (b d s k) -> p b d s k", b=2, d=DH, s=BLOCK)
        dst_rows = c_flat[0:GROUPS, Z2T:Z2T + GROUP].bitcast(I32)
        dst_rows_f = c_flat[0:GROUPS, Z2T + GROUP:Z2T + 2 * GROUP]
        onehot = c_flat[:, Z2T + 3 * GROUP:Z2T + 3 * GROUP + 2 * GROUP_TILES * WIN].rearrange(
            "p (b j n) -> p b j n", b=2, j=GROUP_TILES)
        inv = c_flat[:, Z2T + 4 * GROUP:Z2T + 4 * GROUP + N // 5]
        rows = sb("rows", [P, 2, GROUP_TILES, D])
        src_sb = sb("src_sb", [P, GROUPS, GROUP_TILES], I32)
        src_now = sb("src_now", [P, 2, GROUP_TILES], I32)
        dst_sb = sb("dst_sb", [P, GROUPS, GROUP_TILES], I32)
        rel = sb("rel", [P, GROUPS, GROUP_TILES])
        base_bc = sb("base_bc", [P, GROUPS])
        win = sb("win", [GROUPS, 2])
        win_max = sb("win_max", [GROUPS, 1])
        win_row = sb("win_row", [1, GROUPS, 2])
        base_i = sb("base_i", [1, GROUPS], I32)
        wide_f = sb("wide_f", [1, 1])
        wide_i = sb("wide_i", [1, 1], I32)
        iota = sb("iota", [P, WIN])
        ones = sb("ones", [P, P])
        ident = sb("ident", [P, P])
        w_sb = sb("w_sb", [P, DH, D])
        b_sb = sb("b_sb", [1, D])
        U_sb = sb("U_sb", [P, DH, 3, H])
        V_sb = sb("V_sb", [P, HH, 3, H])
        gb = sb("gb", [P, 3, HH])
        stats = sb("stats", [CHUNKS, STEPS, 6])
        mv = sb("mv", [CHUNKS, STEPS, 2])
        rstd = sb("rstd", [CHUNKS, STEPS])
        var_eps = sb("var_eps", [CHUNKS, STEPS])
        sd = sb("sd", [CHUNKS, STEPS])
        newton = sb("newton", [CHUNKS, STEPS])
        z2 = sb("z2", [CHUNKS, 2, D])
        pre = sb("pre", [P, 2, MT, COLS[0][1]])
        gate = sb("gate", [P, 2, MT, COLS[0][1]])
        ig = sb("ig", [P, 2, HH, COLS[0][1]])
        hc = sb("hc", [P, 2, HH, COLS[0][1]])
        tc = sb("tc", [P, 2, HH, COLS[0][1]])
        gap = U_sb[:, :, :, :].rearrange("p d n h -> p (d n h)")[:, 0:2 * HH * (CHUNKS - 1)].rearrange(
            "p (a m k) -> p a m k", a=2, m=HH)
        near = sb("near", [P, 1])
        far_f = sb("far_f", [1, 1])
        far_i = sb("far_i", [1, 1], I32)

        ps_agg = [ps(f"ps_agg{i}", [P, 512]) for i in range(2)]
        ps_x = [ps(f"ps_x{i}", [P, 512]) for i in range(2)]
        ps_t = [ps(f"ps_t{i}", [P, 512]) for i in range(2)]
        ps_g = [ps(f"ps_g{i}", [P, 512]) for i in range(2)]

        x_in = sem("x_in")
        edges_set = sem("edges_set")
        src_in = sem("src_in")
        dst_in = sem("dst_in")
        dst_rows_in = sem("dst_rows_in")
        weights_in = sem("weights_in")
        ident_zero = sem("ident_zero")
        consts = sem("consts")
        dve_seq = sem("dve_seq")
        z_ready = sem("z_ready")
        z_out = sem("z_out")
        win_ready = sem("win_ready")
        win_out = sem("win_out")
        base_in = sem("base_in")
        wide_ready = sem("wide_ready")
        rows_in = [sem(f"rows_in{i}") for i in range(2 * GROUP_TILES)]
        src_copied = sem("src_copied")
        rows_used = sem("rows_used")
        onehot_ready = sem("onehot_ready")
        agg_added = sem("agg_added")
        mean_ready = sem("mean_ready")
        weights_scaled = sem("weights_scaled")
        msg_ready = sem("msg_ready")
        z2_ready = sem("z2_ready")
        z2T_ps = sem("z2T_ps")
        z2T_ready = sem("z2T_ready")
        gx_ps = sem("gx_ps")
        gx_ready = sem("gx_ready")
        start_set = sem("start_set")
        start_ready = sem("start_ready")
        moved = sem("moved")
        x1_ready = sem("x1_ready")
        var_ready = sem("var_ready")
        sqrt_ready = sem("sqrt_ready")
        ig_ps = [sem(f"ig_ps{i}") for i in range(2)]
        o_ps = [sem(f"o_ps{i}") for i in range(2)]
        ig_pre = [sem(f"ig_pre{i}") for i in range(2)]
        o_pre = [sem(f"o_pre{i}") for i in range(2)]
        ig_gate = [sem(f"ig_gate{i}") for i in range(2)]
        o_gate = [sem(f"o_gate{i}") for i in range(2)]
        hc_ready = [sem(f"hc_ready{i}") for i in range(2)]
        ig_ready = [sem(f"ig_ready{i}") for i in range(2)]
        c_ready = [sem(f"c_ready{i}") for i in range(2)]
        tc_ready = [sem(f"tc_ready{i}") for i in range(2)]
        h_ready = [sem(f"h_ready{i}") for i in range(2)]
        waits_passed = sem("waits_passed")
        near_ready = sem("near_ready")
        near_ps = sem("near_ps")
        far_ready = sem("far_ready")
        hT_ready = sem("hT_ready")
        out_ready = sem("out_ready")
        out_done = sem("out_done")

        WARM = STEPS - WARM_FROM
        ROUNDS = [(WARM_FROM, 0), (0, WARM), (0, WARM + STEPS)]
        DONE = WARM + 2 * STEPS
        N_WEIGHTS = 16 * 11

        block = ctx.enter_context(nc.Block())

        @block.sync
        def _(sp):
            x_rows = x.rearrange("(k s) d -> k s d", s=STEPS)
            sp.dma_start(x_sb[:, :, :], x_rows).then_inc(x_in, 16)
            sp.dma_start(dst_rows[0:GROUPS - 1, :], dst[0:(GROUPS - 1) * GROUP].rearrange("(g e) -> g e", e=GROUP)
                         ).then_inc(dst_rows_in, 16)
            sp.dma_start(dst_rows[GROUPS - 1:GROUPS, 0:TAIL], dst[E - TAIL:E].rearrange("(a e) -> a e", a=1)
                         ).then_inc(dst_rows_in, 16)
            sp.dma_start(dst_rows[GROUPS - 1:GROUPS, TAIL:GROUP],
                         dst[E - (GROUP - TAIL):E].rearrange("(a e) -> a e", a=1)).then_inc(dst_rows_in, 16)
            sp.wait_ge(edges_set, 2)
            for t_sb, t, s in ((dst_sb, dst, dst_in), (src_sb, src, src_in)):
                sp.dma_start(t_sb[:, 0:GROUPS - 1, :],
                             t[0:(GROUPS - 1) * GROUP].rearrange("(g p j) -> p g j", p=P, j=GROUP_TILES)
                             ).then_inc(s, 16)
                sp.dma_start(t_sb[0:TAIL_P, GROUPS - 1, :],
                             t[(GROUPS - 1) * GROUP:E - TAIL_J].rearrange("(p j) -> p j", j=GROUP_TILES)
                             ).then_inc(s, 16)
                sp.dma_start(t_sb[TAIL_P:TAIL_P + 1, GROUPS - 1, 0:TAIL_J],
                             t[E - TAIL_J:E].rearrange("(a j) -> a j", a=1)).then_inc(s, 16)
            sp.wait_ge(win_ready, 1)
            sp.dma_start(win_dram, win[:, :]).then_inc(win_out, 16)
            sp.wait_ge(win_out, 16)
            sp.dma_start(win_row[0:1, :, :], win_dram.rearrange("(a g) c -> a g c", a=1)).then_inc(base_in, 16)
            with nc.allow_non_contiguous_dma("window starts"):
                sp.dma_start(base_bc[:, :], win_dram[:, 0].partition_broadcast(P)).then_inc(base_in, 16)
            sp.wait_ge(z_ready, STEPS)
            sp.dma_start(z_dram.rearrange("(k s) d -> k s d", s=STEPS), z_sb).then_inc(z_out, 16)
            out_rows = out.rearrange("(k s) d -> k s d", s=STEPS)
            for b in range(0, STEPS, 5):
                sp.wait_ge(out_ready, b + 5)
                sp.dma_start(out_rows[:, b:b + 5, :], x_sb[:, b:b + 5, :]).then_inc(out_done, 16)
            sp.wait_ge(out_done, 16 * (STEPS // 5))

        def at_each_round(eng, run_round, count_near=None):
            for n, (first, done) in enumerate(ROUNDS):
                run_round(first, done, n + 1)
            if count_near:
                count_near()
            eng.wait_ge(far_ready, 1)
            far = eng.value_load(far_i[0:1, 0:1], min_val=0, max_val=1)
            with eng.If(far > 0):
                with eng.Fori(0, CHUNKS) as r:
                    run_round(0, r * STEPS + DONE, r + (len(ROUNDS) + 1))

        @block.gpsimd
        def _(pool):
            nc.gpsimd.memset(src_sb[:, :, :], 0).then_inc(edges_set, 1)
            nc.gpsimd.memset(dst_sb[:, :, :], -1).then_inc(edges_set, 1)
            nc.gpsimd.iota(iota[:, :], pattern=[[1, WIN]], base=0, channel_multiplier=0,
                           allow_small_or_imprecise_dtypes=True).then_inc(consts, 1)
            nc.gpsimd.memset(ones[:, :], 1.0).then_inc(consts, 1)
            nc.gpsimd.memset(ident[:, :], 0.0).then_inc(ident_zero, 1)
            pool.wait_ge(ident_zero, 1)
            nc.gpsimd.affine_select(out=ident[:, :], in_=ident[:, :], compare_op=ALU.not_equal, fill=1.0, base=0,
                                    pattern=[[-1, P]], channel_multiplier=1).then_inc(consts, 1)

            src_cols = src_sb[:, :, :].rearrange("p g j -> p (g j)")

            def gather(i, b, turn):
                if turn is not None:
                    pool.wait_ge(rows_used, 2 * turn + (b - 1))
                nc.gpsimd.tensor_copy(src_now[:, b, :], src_cols[:, bass.ds((2 * i + b) * GROUP_TILES, GROUP_TILES)]
                                      ).then_inc(src_copied, 1)
                pool.wait_ge(src_copied, 2 * (0 if turn is None else turn) + (b + 1))
                pool.sem_inc(waits_passed)
                for j in range(GROUP_TILES):
                    pool.indirect_dma_start(
                        rows[:, b, j, :], None, z_dram,
                        bass.IndirectOffsetOnAxis(ap=src_now[:, b, j:j + 1].bitcast(U32), axis=0),
                    ).then_inc(rows_in[b * GROUP_TILES + j], 16)

            pool.wait_ge(src_in, 48)
            pool.wait_ge(z_out, 16)
            for b in range(2):
                gather(0, b, None)
            with pool.Fori(1, PAIRS) as i:
                for b in range(2):
                    gather(i, b, i)
            pool.wait_ge(wide_ready, 1)
            wide = pool.value_load(wide_i[0:1, 0:1], min_val=0, max_val=1)
            with pool.If(wide > 0):
                with pool.Fori(1, PASSES) as n:
                    with pool.Fori(0, PAIRS) as i:
                        for b in range(2):
                            gather(i, b, n * PAIRS + i)

            def run_round(first, done, starts):
                pool.wait_ge(start_ready, starts)
                pool.sem_inc(waits_passed)
                with pool.Fori(first, STEPS) as s:
                    turn = s + (done - first)
                    for q, (c0, c1) in enumerate(COLS):
                        pool.wait_ge(h_ready[q], turn + 1)
                        nc.gpsimd.tensor_tensor(hc[:, q, :, 0:c1 - c0], h_all[:, bass.ds(s, 1), :, c0:c1],
                                                c_all[:, bass.ds(s, 1), :, c0:c1], ALU.mult).then_inc(hc_ready[q], 1)

            at_each_round(pool, run_round)

        @block.scalar
        def _(act):
            for n, (U, V, b) in enumerate(((U_i, V_i, b_i), (U_c, V_c, b_c), (U_o, V_o, b_o))):
                act.dma_start(U_sb[:, :, n, :], U.rearrange("(a p) h -> p a h", p=P)).then_inc(weights_in, 16)
                act.dma_start(V_sb[:, :, n, :], V.rearrange("(a p) h -> p a h", p=P)).then_inc(weights_in, 16)
                with nc.allow_non_contiguous_dma("bias columns"):
                    act.dma_start(gb[:, n, :], b.rearrange("(a p) -> p a", p=P)).then_inc(weights_in, 16)
            act.dma_start(w_sb[:, :, :], w_gnn.rearrange("(a p) h -> p a h", p=P)).then_inc(weights_in, 16)
            act.dma_start(b_sb[:, :], b_gnn.rearrange("(a h) -> a h", a=1)).then_inc(weights_in, 16)

            def deviation(n, s0, s1):
                act.wait_ge(var_ready, n)
                nc.scalar.activation(sd[:, s0:s1], var_eps[:, s0:s1], ACT.Sqrt).then_inc(sqrt_ready, 1)

            deviation(1, 0, STEPS)
            act.wait_ge(weights_scaled, 7)
            tile = 0
            deviation(2, 0, BLOCK)
            for b0 in range(0, STEPS, BLOCK):
                nb = min(BLOCK, STEPS - b0)
                if b0 + nb < STEPS:
                    deviation(b0 // BLOCK + 3, b0 + nb, min(b0 + nb + BLOCK, STEPS))
                for m in range(MT):
                    act.wait_ge(gx_ps, tile + 1)
                    nc.scalar.activation(gx[:, b0:b0 + nb, m, :],
                                         ps_x[tile % 2][:, 0:nb * CHUNKS].rearrange("p (s k) -> p s k", s=nb),
                                         ACT.Identity, bias=gb[:, m // HH, m % HH:m % HH + 1]).then_inc(gx_ready, 1)
                    tile += 1

            def run_round(first, done, starts):
                with act.Fori(first, STEPS) as s:
                    turn = s + (done - first)
                    for q, (c0, c1) in enumerate(COLS):
                        n = c1 - c0
                        act.wait_ge(ig_pre[q], turn + 1)
                        nc.scalar.activation(gate[:, q, 0:2 * HH, 0:n], pre[:, q, 0:2 * HH, 0:n], ACT.Tanh
                                             ).then_inc(ig_gate[q], 1)
                        act.wait_ge(o_pre[q], turn + 1)
                        nc.scalar.activation(gate[:, q, 2 * HH:MT, 0:n], pre[:, q, 2 * HH:MT, 0:n], ACT.Tanh
                                             ).then_inc(o_gate[q], 1)
                        act.wait_ge(c_ready[q], turn + 1)
                        nc.scalar.activation(tc[:, q, :, 0:n], c_all[:, bass.ds(s + 1, 1), :, c0:c1], ACT.Tanh,
                                             scale=0.5).then_inc(tc_ready[q], 1)

            at_each_round(act, run_round)

        @block.tensor
        def _(pe):
            pe.wait_ge(consts, 3)

            def sum_edges(b, turn):
                for j in range(GROUP_TILES):
                    pe.wait_ge(rows_in[b * GROUP_TILES + j], 16 * turn + 16)
                pe.wait_ge(onehot_ready, 2 * turn + (b + 1))
                for d in range(DH + 1):
                    for j in range(GROUP_TILES):
                        lhs = rows[:, b, j, d * P:(d + 1) * P] if d < DH else ones[:, :]
                        mm = nc.tensor.matmul(ps_agg[b][:, d * WIN:(d + 1) * WIN], lhs, onehot[:, b, j, :],
                                              start=(j == 0), stop=(j == GROUP_TILES - 1))
                mm.then_inc(rows_used, 1)

            for b in range(2):
                sum_edges(b, 0)
            with pe.Fori(1, PAIRS) as i:
                for b in range(2):
                    pe.wait_ge(agg_added, 2 * i + (b - 1))
                    sum_edges(b, i)
            pe.wait_ge(wide_ready, 1)
            wide = pe.value_load(wide_i[0:1, 0:1], min_val=0, max_val=1)
            with pe.If(wide > 0):
                with pe.Fori(1, PASSES) as n:
                    with pe.Fori(0, PAIRS) as i:
                        for b in range(2):
                            turn = n * PAIRS + i
                            pe.wait_ge(agg_added, 2 * turn + (b - 1))
                            sum_edges(b, turn)

            pe.wait_ge(mean_ready, 1)
            pe.wait_ge(weights_scaled, 7)

            def message(s):
                if s >= 2:
                    pe.wait_ge(x1_ready, s - 1)
                for d in range(DH):
                    nc.tensor.matmul(ps_agg[s % 2][0:CHUNKS, 0:D], agg[:, d, s:N:STEPS], w_sb[:, d, :],
                                     start=(d == 0), stop=False)
                nc.tensor.matmul(ps_agg[s % 2][0:CHUNKS, 0:D], agg[0:1, DH, s:N:STEPS], b_sb[0:1, :],
                                 start=False, stop=True).then_inc(msg_ready, 1)

            def turn_z2(s):
                pe.wait_ge(z2_ready, s + 1)
                if s >= 2:
                    pe.wait_ge(z2T_ready, s - 1)
                for d in range(DH):
                    mm = nc.tensor.transpose(ps_t[s % 2][:, d * CHUNKS:(d + 1) * CHUNKS],
                                             z2[:, s % 2, d * P:(d + 1) * P], ident[0:CHUNKS, 0:CHUNKS])
                mm.then_inc(z2T_ps, 1)

            tile = 0

            def gates_x(b0):
                nonlocal tile
                nb = min(BLOCK, STEPS - b0)
                pe.wait_ge(z2T_ready, b0 + nb)
                for m in range(MT):
                    if tile >= 2:
                        pe.wait_ge(gx_ready, tile - 1)
                    for d in range(DH):
                        mm = nc.tensor.matmul(ps_x[tile % 2][:, 0:nb * CHUNKS],
                                              U_sb[:, d, m // HH, (m % HH) * P:(m % HH + 1) * P],
                                              z2T[:, (b0 // BLOCK) % 2, d, 0:nb, :].rearrange("p s k -> p (s k)"),
                                              start=(d == 0), stop=(d == DH - 1))
                    mm.then_inc(gx_ps, 1)
                    tile += 1

            for b0 in range(0, STEPS, BLOCK):
                for s in range(b0, min(b0 + BLOCK, STEPS)):
                    message(s)
                if b0 > 0:
                    gates_x(b0 - BLOCK)
                for s in range(b0, min(b0 + BLOCK, STEPS)):
                    turn_z2(s)
            gates_x((STEPS - 1) // BLOCK * BLOCK)

            def run_round(first, done, starts):
                pe.wait_ge(start_ready, starts)
                pe.sem_inc(waits_passed)
                with pe.Fori(first, STEPS) as s:
                    turn = s + (done - first)
                    for q, (c0, c1) in enumerate(COLS):
                        pe.wait_ge(h_ready[q], turn + 1)
                        for m in range(MT):
                            for d in range(HH):
                                bank, at = (ps_g[q], m) if m < 2 * HH else (ps_x[q], m - 2 * HH)
                                mm = nc.tensor.matmul(bank[:, at * (c1 - c0):(at + 1) * (c1 - c0)],
                                                      V_sb[:, d, m // HH, (m % HH) * P:(m % HH + 1) * P],
                                                      h_all[:, bass.ds(s, 1), d, c0:c1],
                                                      start=(d == 0), stop=(d == HH - 1))
                            if m == 2 * HH - 1:
                                mm.then_inc(ig_ps[q], 1)
                        mm.then_inc(o_ps[q], 1)

            def count_near():
                pe.wait_ge(near_ready, 1)
                nc.tensor.matmul(ps_t[0][0:1, 0:1], near[:, :], ones[:, 0:1], start=True, stop=True
                                 ).then_inc(near_ps, 1)

            at_each_round(pe, run_round, count_near)

            for s in range(STEPS):
                if s >= 2:
                    pe.wait_ge(out_ready, s - 1)
                for d in range(HH):
                    mm = nc.tensor.transpose(ps_t[s % 2][0:CHUNKS, d * P:(d + 1) * P], h_all[:, s + 1, d, :],
                                             ident[:, :])
                mm.then_inc(hT_ready, 1)

        @block.vector
        def _(dve):
            seq = [0]

            def link(ins):
                seq[0] += 1
                ins.then_inc(dve_seq, 1)
                dve.wait_ge(dve_seq, seq[0])

            def norm_stats(s, t):
                link(nc.vector.bn_stats(stats[:, s, :], t))
                nc.vector.bn_aggr(mv[:, s, :], stats[:, s, :]).then_inc(dve_seq, 1)
                seq[0] += 1

            sqrts = [0]

            def inverse_deviation(s0, s1):
                ve, y, t = var_eps[:, s0:s1], rstd[:, s0:s1], newton[:, s0:s1]
                nc.vector.tensor_scalar(ve, mv[:, s0:s1, 1], EPS, None, ALU.add).then_inc(var_ready, 1)
                sqrts[0] += 1
                dve.wait_ge(sqrt_ready, sqrts[0])
                link(nc.vector.reciprocal(y, sd[:, s0:s1]))
                link(nc.vector.tensor_tensor(t, y, y, ALU.mult))
                link(nc.vector.tensor_tensor(t, t, ve, ALU.mult))
                link(nc.vector.tensor_scalar(t, t, -0.5, 1.5, ALU.mult, ALU.add))
                link(nc.vector.tensor_tensor(y, y, t, ALU.mult))

            dve.wait_ge(x_in, 16)
            for s in range(STEPS):
                norm_stats(s, x_sb[:, s, :])
            dve.wait_ge(dve_seq, seq[0])
            inverse_deviation(0, STEPS)
            for s in range(STEPS):
                nc.vector.tensor_scalar(z_sb[:, s, :], x_sb[:, s, :], mv[:, s, 0:1], rstd[:, s:s + 1],
                                        ALU.subtract, ALU.mult).then_inc(z_ready, 1)

            dve.wait_ge(dst_rows_in, 48)
            link(nc.vector.tensor_copy(dst_rows_f[:, :], dst_rows[:, :]))
            link(nc.vector.tensor_reduce(win[:, 0:1], dst_rows_f[:, :], AX_X, ALU.min))
            link(nc.vector.tensor_reduce(win_max[:, :], dst_rows_f[:, :], AX_X, ALU.max))
            link(nc.vector.tensor_tensor(win_max[:, :], win_max[:, :], win[:, 0:1], ALU.subtract))
            nc.vector.tensor_scalar(win[:, 1:2], win_max[:, :], float(WIN), None, ALU.is_ge).then_inc(win_ready, 1)
            nc.vector.memset(agg[:, :, :], 0.0).then_inc(dve_seq, 1)
            seq[0] += 1
            dve.wait_ge(dve_seq, seq[0])
            dve.wait_ge(base_in, 32)
            link(nc.vector.tensor_reduce(wide_f[:, :], win_row[0:1, :, 1], AX_X, ALU.max))
            nc.vector.tensor_copy(wide_i[:, :], wide_f[:, :]).then_inc(wide_ready, 1)
            link(nc.vector.tensor_copy(base_i[:, :], win_row[0:1, :, 0]))
            dve.wait_ge(dst_in, 48)
            link(nc.vector.tensor_tensor(rel[:, :, :], dst_sb[:, :, :],
                                         base_bc[:, :].unsqueeze(2).to_broadcast([P, GROUPS, GROUP_TILES]),
                                         ALU.subtract))
            dve.wait_ge(consts, 1)

            def targets(i, b):
                nc.vector.tensor_tensor(
                    onehot[:, b, :, :], iota[:, :].unsqueeze(1).to_broadcast([P, GROUP_TILES, WIN]),
                    rel[:, bass.ds(2 * i + b, 1), :].rearrange("p a j -> p (a j)").unsqueeze(2).to_broadcast(
                        [P, GROUP_TILES, WIN]),
                    ALU.is_equal).then_inc(onehot_ready, 1)

            def add_sums(i, b, turn):
                base = dve.value_load(base_i[0:1, bass.ds(2 * i + b, 1)], min_val=0, max_val=N)
                dve.wait_ge(rows_used, 2 * turn + (b + 1))
                nc.vector.tensor_tensor(agg[:, :, bass.ds(base, WIN)], agg[:, :, bass.ds(base, WIN)],
                                        ps_agg[b][:, 0:(DH + 1) * WIN].rearrange("p (d n) -> p d n", n=WIN),
                                        ALU.add).then_inc(agg_added, 1)
                dve.wait_ge(agg_added, 2 * turn + (b + 1))

            for b in range(2):
                targets(0, b)
            with dve.Fori(1, PAIRS) as i:
                for b in range(2):
                    add_sums(i - 1, b, i - 1)
                    targets(i, b)
            for b in range(2):
                add_sums(PAIRS - 1, b, PAIRS - 1)
            wide = dve.value_load(wide_i[0:1, 0:1], min_val=0, max_val=1)
            with dve.If(wide > 0):
                with dve.Fori(1, PASSES) as n:
                    nc.vector.tensor_scalar(rel[:, :, :], rel[:, :, :], -float(WIN), None, ALU.add
                                            ).then_inc(moved, 1)
                    nc.vector.tensor_scalar(base_i[:, :], base_i[:, :], WIN, N, ALU.add, ALU.min
                                            ).then_inc(moved, 1)
                    dve.wait_ge(moved, 2 * n)
                    dve.sem_inc(waits_passed)
                    with dve.Fori(0, PAIRS) as i:
                        for b in range(2):
                            targets(i, b)
                            add_sums(i, b, n * PAIRS + i)

            for n0 in range(0, N, N // 5):
                nn = slice(n0, n0 + N // 5)
                link(nc.vector.tensor_scalar(inv[:, :], agg[:, DH, nn], 1.0, None, ALU.max))
                link(nc.vector.reciprocal(inv[:, :], inv[:, :]))
                link(nc.vector.tensor_tensor(agg[:, 0:DH, nn], agg[:, 0:DH, nn],
                                             inv[:, :].unsqueeze(1).to_broadcast([P, DH, N // 5]), ALU.mult))
            nc.vector.tensor_scalar(agg[:, DH, 0:N], agg[:, DH, 0:N], 1.0, None, ALU.min).then_inc(mean_ready, 1)

            dve.wait_ge(weights_in, N_WEIGHTS)
            for n, half in ((0, 0.5), (2, 0.5)):
                nc.vector.tensor_scalar(U_sb[:, :, n, :], U_sb[:, :, n, :], half, None, ALU.mult
                                        ).then_inc(weights_scaled, 1)
                nc.vector.tensor_scalar(gb[:, n, :], gb[:, n, :], half, None, ALU.mult).then_inc(weights_scaled, 1)
                nc.vector.tensor_scalar(V_sb[:, :, n, :], V_sb[:, :, n, :], half * 0.5, None, ALU.mult
                                        ).then_inc(weights_scaled, 1)
            nc.vector.tensor_scalar(V_sb[:, :, 1, :], V_sb[:, :, 1, :], 0.5, None, ALU.mult).then_inc(weights_scaled, 1)

            for b0 in range(0, STEPS, BLOCK):
                b1 = min(b0 + BLOCK, STEPS)
                for s in range(b0, b1):
                    dve.wait_ge(msg_ready, s + 1)
                    nc.vector.tensor_tensor(x_sb[:, s, :], x_sb[:, s, :], ps_agg[s % 2][0:CHUNKS, 0:D], ALU.add
                                            ).then_inc(x1_ready, 1)
                    dve.wait_ge(x1_ready, s + 1)
                    norm_stats(s, x_sb[:, s, :])
                dve.wait_ge(dve_seq, seq[0])
                inverse_deviation(b0, b1)
                for s in range(b0, b1):
                    if s >= 2:
                        dve.wait_ge(z2T_ps, s - 1)
                    nc.vector.tensor_scalar(z2[:, s % 2, :], x_sb[:, s, :], mv[:, s, 0:1], rstd[:, s:s + 1],
                                            ALU.subtract, ALU.mult).then_inc(z2_ready, 1)
                    for t in ([s - 1] if s > b0 else []) + ([s] if s == b1 - 1 else []):
                        dve.wait_ge(z2T_ps, t + 1)
                        if t >= 2 * BLOCK and t % BLOCK == 0:
                            dve.wait_ge(gx_ps, MT * (t // BLOCK - 1))
                        nc.vector.tensor_copy(z2T[:, (t // BLOCK) % 2, :, t % BLOCK, :],
                                              ps_t[t % 2][:, 0:DH * CHUNKS].rearrange("p (d k) -> p d k", d=DH)
                                              ).then_inc(z2T_ready, 1)

            dve.wait_ge(gx_ready, MT * -(-STEPS // BLOCK))
            nc.vector.memset(c_all[:, WARM_FROM, :, :], 0.0).then_inc(start_set, 1)
            nc.vector.memset(h_all[:, 0, :, 0:1], 0.0).then_inc(start_set, 1)
            nc.vector.memset(c_all[:, 0, :, 0:1], 0.0).then_inc(start_set, 1)
            for q, (c0, c1) in enumerate(COLS):
                nc.vector.memset(h_all[:, WARM_FROM, :, c0:c1], 0.0).then_inc(h_ready[q], 1)
                dve.wait_ge(h_ready[q], 1)
            dve.wait_ge(start_set, 3)
            nc.vector.memset(far_f[:, :], 0.0).then_inc(start_ready, 1)

            def run_round(first, done, starts):
                if first == 0:
                    for q in range(2):
                        dve.wait_ge(h_ready[q], done + 1)
                    nc.vector.tensor_copy(h_all[:, 0, :, 1:CHUNKS], h_all[:, STEPS, :, 0:CHUNKS - 1]
                                          ).then_inc(start_set, 1)
                    nc.vector.tensor_copy(c_all[:, 0, :, 1:CHUNKS], c_all[:, STEPS, :, 0:CHUNKS - 1]
                                          ).then_inc(start_ready, 1)
                    dve.wait_ge(start_ready, starts)
                    dve.sem_inc(waits_passed)
                with dve.Fori(first, STEPS) as s:
                    turn = s + (done - first)
                    for q, (c0, c1) in enumerate(COLS):
                        n = c1 - c0
                        v_ig = ps_g[q][:, 0:2 * HH * n].rearrange("p (m k) -> p m k", k=n)
                        v_o = ps_x[q][:, 0:HH * n].rearrange("p (m k) -> p m k", k=n)
                        now = bass.ds(s, 1)
                        then = bass.ds(s + 1, 1)
                        dve.wait_ge(ig_ps[q], turn + 1)
                        nc.vector.tensor_tensor(pre[:, q, 0:2 * HH, 0:n], v_ig,
                                                gx[:, now, 0:2 * HH, c0:c1], ALU.add).then_inc(ig_pre[q], 1)
                        dve.wait_ge(o_ps[q], turn + 1)
                        nc.vector.tensor_tensor(pre[:, q, 2 * HH:MT, 0:n], v_o,
                                                gx[:, now, 2 * HH:MT, c0:c1], ALU.add).then_inc(o_pre[q], 1)
                        dve.wait_ge(ig_gate[q], turn + 1)
                        nc.vector.scalar_tensor_tensor(out=ig[:, q, :, 0:n], in0=gate[:, q, 0:HH, 0:n], scalar=1.0,
                                                       in1=gate[:, q, HH:2 * HH, 0:n], op0=ALU.add, op1=ALU.mult
                                                       ).then_inc(ig_ready[q], 1)
                        dve.wait_ge(ig_ready[q], turn + 1)
                        dve.wait_ge(hc_ready[q], turn + 1)
                        nc.vector.scalar_tensor_tensor(out=c_all[:, then, :, c0:c1], in0=hc[:, q, :, 0:n], scalar=0.5,
                                                       in1=ig[:, q, :, 0:n], op0=ALU.mult, op1=ALU.add
                                                       ).then_inc(c_ready[q], 1)
                        dve.wait_ge(tc_ready[q], turn + 1)
                        nc.vector.scalar_tensor_tensor(out=h_all[:, then, :, c0:c1], in0=gate[:, q, 2 * HH:MT, 0:n],
                                                       scalar=1.0, in1=tc[:, q, :, 0:n], op0=ALU.add, op1=ALU.mult
                                                       ).then_inc(h_ready[q], 1)

            def count_near():
                for q in range(2):
                    dve.wait_ge(h_ready[q], DONE + 1)
                for n, state in enumerate((h_all, c_all)):
                    link(nc.vector.tensor_tensor(gap[:, n, :, :], state[:, STEPS, :, 0:CHUNKS - 1],
                                                 state[:, 0, :, 1:CHUNKS], ALU.subtract))
                link(nc.vector.tensor_tensor(gap, gap, gap, ALU.mult))
                link(nc.vector.tensor_scalar(gap, gap, STATE_TOL ** 2, None, ALU.is_le))
                nc.vector.tensor_reduce(near[:, :], gap.rearrange("p a m k -> p (a m k)"), AX_X, ALU.add
                                        ).then_inc(near_ready, 1)
                dve.wait_ge(near_ps, 1)
                link(nc.vector.tensor_scalar(far_f[:, :], ps_t[0][0:1, 0:1], float(P * 2 * HH * (CHUNKS - 1)), None,
                                             ALU.is_lt))
                nc.vector.tensor_copy(far_i[:, :], far_f[:, :]).then_inc(far_ready, 1)

            at_each_round(dve, run_round, count_near)

            for s in range(STEPS):
                dve.wait_ge(hT_ready, s + 1)
                nc.vector.scalar_tensor_tensor(out=x_sb[:, s, :], in0=ps_t[s % 2][0:CHUNKS, 0:H], scalar=0.5,
                                               in1=x_sb[:, s, :], op0=ALU.mult, op1=ALU.add).then_inc(out_ready, 1)


_INS = ['x', 'src', 'dst', 'L0_gnn_weight', 'L0_gnn_bias', 'L0_ffn_U_i', 'L0_ffn_V_i', 'L0_ffn_b_i',
        'L0_ffn_U_c', 'L0_ffn_V_c', 'L0_ffn_b_c', 'L0_ffn_U_o', 'L0_ffn_V_o', 'L0_ffn_b_o']


def kernel(**inputs):
    import numpy as _np
    import concourse.bacc as _bacc
    from concourse import mybir as _mybir
    from concourse.bass_utils import run_bass_kernel_spmd as _run

    nc = _bacc.Bacc("TRN2", target_bir_lowering=False, num_devices=1)
    arrays, args = {}, []
    for name in _INS:
        a = _np.ascontiguousarray(inputs[name])
        arrays[f"in_{name}_dram"] = a
        args.append(nc.dram_tensor(f"in_{name}_dram", a.shape, _mybir.dt.from_np(a.dtype), kind="ExternalInput").ap())
    args.append(nc.dram_tensor("out_0_dram", inputs["x"].shape, _mybir.dt.float32, kind="ExternalOutput").ap())
    bass_gnn_lstm_kernel(nc, *args)
    r = _run(nc, [arrays], core_ids=[0])
    return r.results[0]["out_0_dram"]
```

```python
from contextlib import ExitStack

import concourse.bass as bass
from concourse import mybir

F32 = mybir.dt.float32
I32 = mybir.dt.int32
U32 = mybir.dt.uint32
F16 = mybir.dt.float16
ALU = mybir.AluOpType
ACT = mybir.ActivationFunctionType
AX_X = mybir.AxisListType.X

P = 128
EPS = 1e-5

NODE_BLOCK = 125
WINDOWS = 11
WIN_TILES = 2
POOL_SHARE = (1, 2)

STEPS = 25
WARM_FROM = 4
UNROLL = 4
STATE_TOL = 2.0 ** -18


def bass_gnn_lstm_kernel(nc, x, src, dst, w_gnn, b_gnn, U_i, V_i, b_i, U_c, V_c, b_c, U_o, V_o, b_o, out):
    N, D = x.shape
    E = src.shape[0]
    H = U_i.shape[1]
    DH = D // P
    HH = H // P
    CHUNKS = N // STEPS
    NB = NODE_BLOCK
    BLOCKS = N // NB
    CPB = NB // STEPS
    EDGE_ROWS = 125
    EDGE_COLS = E // EDGE_ROWS
    WIN_EDGES = WIN_TILES * P
    NW = BLOCKS * WINDOWS
    WIN_BATCHES = -(-NW // P)
    WIN_ROWS = -(-NW // WIN_BATCHES)
    NWP = WIN_BATCHES * WIN_ROWS
    SPAN = [NB * (w + 1) // WINDOWS - NB * w // WINDOWS for w in range(NW)]
    WIN_MAX = max(SPAN)
    LINE = 2 * D + 2
    MT = 3 * HH
    G_RUN = 8
    X_CHUNK = 5
    COLS = [(0, (CHUNKS + 1) // 2), ((CHUNKS + 1) // 2, CHUNKS)]
    assert N == CHUNKS * STEPS == BLOCKS * NB and NB == CPB * STEPS and CHUNKS <= P
    assert D == DH * P and H == HH * P and D == H
    assert EDGE_COLS % 2 == 1
    assert E == EDGE_ROWS * EDGE_COLS and BLOCKS % X_CHUNK == 0 and WIN_MAX * BLOCKS <= 512 and NWP <= 512

    h_dram = nc.dram_tensor("h_dram", (N, LINE), F16, kind="Internal").ap()

    with ExitStack() as ctx:
        def sb(name, shape, dt=F32):
            return ctx.enter_context(nc.sbuf_tensor(name, shape, dt))

        def ps(name, shape, dt=F32):
            return ctx.enter_context(nc.psum_tensor(name, shape, dt))

        def sem(name):
            return ctx.enter_context(nc.semaphore(name))

        x_sb = sb("x_sb", [NB, BLOCKS, D])
        gx = sb("gx", [P, STEPS, MT, CHUNKS])
        gx_flat = gx[:, :, :, :].rearrange("p s m k -> p (s m k)")
        at = [0]

        def early(parts, n, dt=F32):
            a = gx_flat[0:parts, at[0]:at[0] + n]
            at[0] += n
            return a if dt == F32 else a.bitcast(dt)
        dst_rows = early(EDGE_ROWS, EDGE_COLS, I32)
        first_row = early(EDGE_ROWS, 1)
        before = early(EDGE_ROWS, NWP)
        row_f = early(WIN_ROWS, WIN_BATCHES)
        row_i = early(WIN_ROWS, WIN_BATCHES, I32)
        win_rows = early(WIN_ROWS, WIN_BATCHES * EDGE_COLS, I32).rearrange("p (b e) -> p b e", b=WIN_BATCHES)
        win_rows_f = early(WIN_ROWS, WIN_BATCHES * EDGE_COLS).rearrange("p (b e) -> p b e", b=WIN_BATCHES)
        in_row = early(WIN_ROWS, WIN_BATCHES)
        start_f = early(WIN_ROWS, WIN_BATCHES)
        start_i = early(WIN_ROWS, WIN_BATCHES, I32)
        win_edges = early(WIN_ROWS, 2 * WIN_BATCHES * WIN_EDGES, I32).rearrange(
            "p (a b e) -> p a b e", a=2, b=WIN_BATCHES)
        win_edges_f = early(WIN_ROWS, 2 * WIN_BATCHES * WIN_EDGES).rearrange(
            "p (a b e) -> p a b e", a=2, b=WIN_BATCHES)
        col_thr = early(WIN_ROWS, WIN_BATCHES)
        row_thr = early(P, NWP + 1)
        limit = early(P, NWP)
        rel = early(P, WIN_TILES * NWP).rearrange("p (t w) -> p t w", t=WIN_TILES)
        slot = early(P, WIN_TILES * NWP).rearrange("p (t w) -> p t w", t=WIN_TILES)
        inside = early(P, WIN_TILES * NWP).rearrange("p (t w) -> p t w", t=WIN_TILES)
        z = early(NB, 3 * D).rearrange("p (b d) -> p b d", b=3)
        zT = early(P, 3 * DH * NB, F16).rearrange("p (b c d n) -> p b c d n", b=3, c=2, d=DH)
        w_sb = early(P, DH * D).rearrange("p (d h) -> p d h", d=DH)
        h_all = sb("h_all", [P, STEPS + 1, HH, CHUNKS])
        c_all = sb("c_all", [P, STEPS + 1, HH, CHUNKS])
        h_flat = h_all[:, :, :, :].rearrange("p s m k -> p (s m k)")
        c_flat = c_all[:, :, :, :].rearrange("p s m k -> p (s m k)")
        gap = sb("gap", [P, 2, HH, CHUNKS - 1])
        line = c_flat[0:NB, 0:BLOCKS * LINE // 2].bitcast(F16).rearrange("p (j f) -> p j f", f=LINE)
        U_sb = h_flat[:, 0:DH * 3 * H].rearrange("p (d n h) -> p d n h", d=DH, n=3)
        V_sb = h_flat[:, DH * 3 * H:(DH + HH) * 3 * H].rearrange("p (d n h) -> p d n h", d=HH, n=3)
        at[0] = 0

        def general(n, dt=F32):
            at[0] += n
            a = h_flat[0:EDGE_ROWS, at[0] - n:at[0]]
            return a if dt == F32 else a.bitcast(dt)
        g_dst = general(EDGE_COLS, I32)
        g_src = general(EDGE_COLS, I32)
        g_dst_f = general(EDGE_COLS)
        g_rel = general(EDGE_COLS)
        g_src_now = general(2, I32)
        g_hot = general(P, F16).rearrange("p (b n) -> p b n", b=2)
        g_rows = general(LINE, F16).rearrange("p (b f) -> p b f", b=2)
        counts_all = sb("counts", [P, 2, BLOCKS, P], F16)
        counts = counts_all[0:NB, :, :, :]
        HOTS = 6
        hot_p = sb("hot_p", [P, HOTS, WIN_TILES, P], F16)
        hot_ts = sb("hot_ts", [P, HOTS, WIN_TILES, WIN_MAX * BLOCKS + 4], F16)
        key = sb("key", [P, WIN_TILES, NWP])
        part = sb("part", [P, WIN_TILES, NWP])
        iota = sb("iota", [P, 512], F16)
        covered = sb("covered", [P, 1])
        open_f = sb("open_f", [1, 1])
        open_i = sb("open_i", [1, 1], I32)
        ones = sb("ones", [P, 1])
        ident = sb("ident", [P, P])
        b_bc = sb("b_bc", [NB, D])
        has = sb("has", [NB, 1])
        inv = sb("inv", [NB, 1])
        W16 = sb("W16", [P, 2, DH, D], F16)
        U16 = sb("U16", [P, 2, DH, 3 * H], F16)
        V16 = sb("V16", [P, 2, HH, 3 * H], F16)
        w_max = sb("w_max", [P, 3])
        w_min = sb("w_min", [P, 3])
        w_top = sb("w_top", [P, 3])
        w_exp = sb("w_exp", [P, 3], I32)
        w_scale = sb("w_scale", [P, 3])
        w_unscale = sb("w_unscale", [P, 3])
        h16 = sb("h16", [P, 2, HH, CHUNKS], F16)
        gb = sb("gb", [P, 3, HH])
        stats = sb("stats", [NB, BLOCKS, 6])
        mv = sb("mv", [NB, BLOCKS, 2])
        rstd = sb("rstd", [NB, BLOCKS])
        var_eps = sb("var_eps", [NB, BLOCKS])
        sd = sb("sd", [NB, BLOCKS])
        newton = sb("newton", [NB, BLOCKS])
        z2 = sb("z2", [NB, 2, D])
        TB = 4
        z2T = sb("z2T", [P, 2, 2, DH, TB, NB], F16)
        at[0] = 0
        half = counts_all[:, :, :, :].rearrange("p b s n -> p (b s n)").bitcast(F32)

        def of_step(m):
            n = 2 * m * COLS[0][1]
            at[0] += n
            return half[:, at[0] - n:at[0]].rearrange("p (q m k) -> p q m k", q=2, m=m)
        pre, gate, ig, hc, tc = of_step(MT), of_step(MT), of_step(HH), of_step(HH), of_step(HH)
        h_out = half[:, at[0]:at[0] + 3 * HH * NB].rearrange("p (b m n) -> p b m n", b=3, m=HH)
        near = sb("near", [P, 1])
        far_f = sb("far_f", [1, 1])
        far_i = sb("far_i", [1, 1], I32)

        bank = [ps(f"bank{i}", [P, 512]) for i in range(8)]
        ps_count = [bank[2], bank[3], bank[4]]
        ps_sum = [bank[0], bank[1]]
        ps_zT = bank[5]
        ps_gates = [bank[6], bank[7]]
        ps_g = [bank[0], bank[1]]
        ps_x = [bank[6], bank[7]]
        ps_t = [bank[2], bank[3]]

        x_in = [sem(f"x_in{c}") for c in range(BLOCKS // X_CHUNK)]
        dst_rows_in = sem("dst_rows_in")
        w_in = sem("w_in")
        weights_in = sem("weights_in")
        b_in = sem("b_in")
        ident_zero = sem("ident_zero")
        iotas = sem("iotas")
        consts = sem("consts")
        dve_seq = sem("dve_seq")
        before_ready = sem("before_ready")
        before_ps = sem("before_ps")
        rows_known = sem("rows_known")
        win_rows_in = [sem(f"win_rows_in{b}") for b in range(WIN_BATCHES)]
        starts_known = sem("starts_known")
        win_edges_in = [[sem(f"win_edges_in{a}_{b}") for b in range(WIN_BATCHES)] for a in range(2)]
        edges_f = sem("edges_f")
        edges_ps = sem("edges_ps")
        keys_ready = sem("keys_ready")
        covered_ready = sem("covered_ready")
        covered_ps = sem("covered_ps")
        open_ready = sem("open_ready")
        w_max_ready = sem("w_max_ready")
        w_max_all = sem("w_max_all")
        scales_ready = sem("scales_ready")
        w_hi = sem("w_hi")
        w_split = sem("w_split")
        uv_hi = sem("uv_hi")
        uv_split = sem("uv_split")
        var_ready = sem("var_ready")
        sqrt_ready = sem("sqrt_ready")
        z_ready = sem("z_ready")
        zT_ps = sem("zT_ps")
        zT_hi = sem("zT_hi")
        zT_ready = sem("zT_ready")
        line_ps = sem("line_ps")
        line_hi = sem("line_hi")
        line_ready = sem("line_ready")
        hot_p_pool = sem("hot_p_pool")
        hot_ready = sem("hot_ready")
        count_ps = sem("count_ps")
        counted = sem("counted")
        sum_ps = sem("sum_ps")
        x1_ready = sem("x1_ready")
        z2_ready = sem("z2_ready")
        z2T_ps = sem("z2T_ps")
        z2T_hi = sem("z2T_hi")
        z2T_ready = sem("z2T_ready")
        gx_ps = sem("gx_ps")
        gx_ready = sem("gx_ready")
        h_out_ready = sem("h_out_ready")
        g_in = sem("g_in")
        g_line_out = sem("g_line_out")
        g_seq = sem("g_seq")
        g_src_copied = sem("g_src_copied")
        g_rows_in = [[sem(f"g_rows_in{r}_{b}") for b in range(2)] for r in range(-(-BLOCKS // G_RUN))]
        g_hot_ready = sem("g_hot_ready")
        g_used = sem("g_used")
        start_set = sem("start_set")
        start_ready = sem("start_ready")
        ig_ps = [sem(f"ig_ps{i}") for i in range(2)]
        o_ps = [sem(f"o_ps{i}") for i in range(2)]
        ig_pre = [sem(f"ig_pre{i}") for i in range(2)]
        o_pre = [sem(f"o_pre{i}") for i in range(2)]
        ig_gate = [sem(f"ig_gate{i}") for i in range(2)]
        o_gate = [sem(f"o_gate{i}") for i in range(2)]
        hc_ready = [sem(f"hc_ready{i}") for i in range(2)]
        ig_ready = [sem(f"ig_ready{i}") for i in range(2)]
        c_ready = [sem(f"c_ready{i}") for i in range(2)]
        tc_ready = [sem(f"tc_ready{i}") for i in range(2)]
        h_ready = [sem(f"h_ready{i}") for i in range(2)]
        hi_ready = [sem(f"hi_ready{i}") for i in range(2)]
        lo_ready = [sem(f"lo_ready{i}") for i in range(2)]
        waits_passed = sem("waits_passed")
        near_ready = sem("near_ready")
        near_ps = sem("near_ps")
        far_ready = sem("far_ready")
        hT_ready = sem("hT_ready")
        out_ready = sem("out_ready")
        out_done = sem("out_done")

        WARM = STEPS - WARM_FROM
        ROUNDS = [(WARM_FROM, 0), (0, WARM), (0, WARM + STEPS)]
        DONE = WARM + 2 * STEPS
        PRODUCTS = [(0, 0), (1, 0), (0, 1)]
        LAG = 6
        FINISH_AT, ROOT_AT, NORM_AT, TURN_AT, HIGH_AT, LOW_AT = (7, 2), (8, 2), (3, 3), (4, 3), (5, 3), (0, 4)
        ROUND = 3.0 * 2.0 ** 22
        BATCHES = [(b, min(b + TB, BLOCKS)) for b in range(0, BLOCKS, TB)]

        def on_pool(w):
            return (w * POOL_SHARE[0]) % POOL_SHARE[1] < POOL_SHARE[0]

        def gates_at(j, i):
            return [(b, (j0, j1), m) for b, (j0, j1) in enumerate(BATCHES) for m in range(MT)
                    if (j, i) == (j1 + 3 + m // 2, (1, 6)[m % 2])]

        def where_open(eng, run_block, start=None):
            eng.wait_ge(open_ready, 1)
            with eng.If(eng.value_load(open_i[0:1, 0:1], min_val=0, max_val=1) > 0):
                if start:
                    start()
                for j in range(BLOCKS):
                    run_block(j)

        def tiles_of(eng, one):
            one(0, 0)
            with eng.Fori(0, (EDGE_COLS - 3) // 2) as i:
                one(i * 2 + 1, 1)
                one(i * 2 + 2, 0)
            one(EDGE_COLS - 2, 1)
            one(EDGE_COLS - 1, 0)

        block = ctx.enter_context(nc.Block())

        @block.sync
        def _(sp):
            sp.dma_start(dst_rows, dst.rearrange("(r c) -> r c", c=EDGE_COLS)).then_inc(dst_rows_in, 16)
            x_rows = x.rearrange("(j p) d -> p j d", p=NB)
            for c in range(BLOCKS // X_CHUNK):
                js = slice(c * X_CHUNK, (c + 1) * X_CHUNK)
                sp.dma_start(x_sb[:, js, :], x_rows[:, js, :]).then_inc(x_in[c], 16)
            with nc.allow_non_contiguous_dma("bias to every partition"):
                sp.dma_start(b_bc[:, :], b_gnn.partition_broadcast(NB)).then_inc(b_in, 16)
            sp.wait_ge(open_ready, 1)
            with sp.If(sp.value_load(open_i[0:1, 0:1], min_val=0, max_val=1) > 0):
                sp.wait_ge(gx_ready, MT * len(BATCHES))
                sp.dma_start(h_dram.rearrange("(j p) f -> p j f", p=NB), line).then_inc(g_line_out, 16)
                sp.dma_start(x_sb[:, :, :], x_rows).then_inc(g_in, 16)
                sp.dma_start(g_dst, dst.rearrange("(r c) -> r c", c=EDGE_COLS)).then_inc(g_in, 16)
                sp.dma_start(g_src, src.rearrange("(r c) -> r c", c=EDGE_COLS)).then_inc(g_in, 16)
            out_rows = out.rearrange("(j p) d -> p j d", p=NB)
            for c in range(BLOCKS // X_CHUNK):
                js = slice(c * X_CHUNK, (c + 1) * X_CHUNK)
                sp.wait_ge(out_ready, (c + 1) * X_CHUNK)
                sp.dma_start(out_rows[:, js, :], x_sb[:, js, :]).then_inc(out_done, 16)
            sp.wait_ge(out_done, 16 * (BLOCKS // X_CHUNK))

        def steps_of(eng, first, done):
            if isinstance(done, int):
                yield from range(first + 1, STEPS - UNROLL + 1, UNROLL)
            else:
                with eng.Fori(first + 1, STEPS - UNROLL + 1, UNROLL) as s:
                    yield s

        def at_each_round(eng, run_round, count_near=None):
            for n, (first, done) in enumerate(ROUNDS):
                run_round(first, done, n + 1)
            if count_near:
                count_near()
            eng.wait_ge(far_ready, 1)
            far = eng.value_load(far_i[0:1, 0:1], min_val=0, max_val=1)
            with eng.If(far > 0):
                with eng.Fori(0, CHUNKS) as r:
                    run_round(0, r * STEPS + DONE, r + (len(ROUNDS) + 1))

        @block.gpsimd
        def _(pool):
            nc.gpsimd.iota(row_thr, pattern=[[1, NWP + 1]], base=0, channel_multiplier=0,
                           allow_small_or_imprecise_dtypes=True).then_inc(iotas, 1)
            nc.gpsimd.iota(col_thr, pattern=[[WIN_ROWS, WIN_BATCHES]], base=0, channel_multiplier=1,
                           allow_small_or_imprecise_dtypes=True).then_inc(iotas, 1)
            nc.gpsimd.memset(ones[:, :], 1.0).then_inc(consts, 1)
            nc.gpsimd.memset(ident[:, :], 0.0).then_inc(ident_zero, 1)
            pool.wait_ge(ident_zero, 1)
            nc.gpsimd.affine_select(out=ident[:, :], in_=ident[:, :], compare_op=ALU.not_equal, fill=1.0, base=0,
                                    pattern=[[-1, P]], channel_multiplier=1).then_inc(consts, 1)
            nc.gpsimd.iota(iota[:, :], pattern=[[1, 512]], base=0, channel_multiplier=0,
                           allow_small_or_imprecise_dtypes=True).then_inc(consts, 1)
            nc.gpsimd.memset(counts, 0.0).then_inc(consts, 1)
            nc.gpsimd.memset(line[:, :, 2 * D:LINE], 1.0).then_inc(consts, 1)
            pool.wait_ge(rows_known, 1)
            for b in range(WIN_BATCHES):
                pool.indirect_dma_start(
                    win_rows[:, b, :], None, dst.rearrange("(r c) -> r c", c=EDGE_COLS),
                    bass.IndirectOffsetOnAxis(ap=row_i[:, b:b + 1].bitcast(U32), axis=0),
                ).then_inc(win_rows_in[b], 16)
            pool.wait_ge(w_max_ready, 1)
            nc.gpsimd.partition_all_reduce(w_top[:, :], w_max[:, :], P, bass.bass_isa.ReduceOp.max
                                           ).then_inc(w_max_all, 1)
            pool.wait_ge(starts_known, 1)
            for a, t in enumerate((dst, src)):
                for b in range(WIN_BATCHES):
                    pool.indirect_dma_start(
                        win_edges[:, a, b, :], None,
                        t.rearrange("(e a) -> e a", a=1),
                        bass.IndirectOffsetOnAxis(ap=start_i[:, b:b + 1].bitcast(U32), axis=0),
                    ).then_inc(win_edges_in[a][b], 16)
            pool.wait_ge(keys_ready, 1)
            for w in range(NW):
                if on_pool(w):
                    if w >= HOTS:
                        pool.wait_ge(count_ps, w - HOTS + 1)
                    for t in range(WIN_TILES):
                        ins = nc.gpsimd.tensor_scalar(hot_p[:, w % HOTS, t, :], iota[:, 0:P], part[:, t, w:w + 1], None,
                                                      ALU.is_equal)
                    ins.then_inc(hot_p_pool, 1)

            def general_block(j):
                if j == 0:
                    pool.wait_ge(g_line_out, 16)
                    pool.wait_ge(g_in, 48)

                def one(e, b):
                    turn = e + j * EDGE_COLS
                    if not isinstance(e, int) or turn >= 2:
                        pool.wait_ge(g_used, turn - (0 if isinstance(e, int) and e == 0 else 1))
                        pool.sem_inc(waits_passed)
                    nc.gpsimd.tensor_copy(g_src_now[:, b:b + 1], g_src[:, bass.ds(e, 1)]).then_inc(g_src_copied, 1)
                    pool.wait_ge(g_src_copied, turn + 1)
                    pool.sem_inc(waits_passed)
                    pool.indirect_dma_start(
                        g_rows[:, b, :], None, h_dram,
                        bass.IndirectOffsetOnAxis(ap=g_src_now[:, b:b + 1].bitcast(U32), axis=0),
                    ).then_inc(g_rows_in[j // G_RUN][b], 16)
                tiles_of(pool, one)

            where_open(pool, general_block)

            def low_part(q, slot, seen):
                c0, c1 = COLS[q]
                pool.wait_ge(h_ready[q], seen)
                pool.wait_ge(hi_ready[q], seen)
                nc.gpsimd.tensor_tensor(h16[:, 1, :, c0:c1], h_all[:, slot, :, c0:c1], h16[:, 0, :, c0:c1],
                                        ALU.subtract).then_inc(lo_ready[q], 1)

            def old_part(q, slot):
                c0, c1 = COLS[q]
                nc.gpsimd.tensor_tensor(hc[:, q, :, 0:c1 - c0], h_all[:, slot, :, c0:c1], c_all[:, slot, :, c0:c1],
                                        ALU.mult).then_inc(hc_ready[q], 1)

            def run_round(first, done, starts):
                pool.wait_ge(start_ready, starts)
                pool.sem_inc(waits_passed)

                def step(s, seen):
                    old_part(0, bass.ds(s, 1))
                    low_part(1, bass.ds(s, 1), seen)
                    old_part(1, bass.ds(s, 1))
                    low_part(0, bass.ds(s + 1, 1), seen + 1)

                low_part(0, slice(first, first + 1), done + starts)
                step(first, done + starts)
                for s in steps_of(pool, first, done):
                    for u in range(UNROLL):
                        step(s + u, s + (done - first + starts + u))

            at_each_round(pool, run_round)

        @block.scalar
        def _(act):
            act.dma_start(w_sb, w_gnn.rearrange("(a p) h -> p a h", p=P)).then_inc(w_in, 16)
            for n, (U, V, b) in enumerate(((U_i, V_i, b_i), (U_c, V_c, b_c), (U_o, V_o, b_o))):
                act.dma_start(U_sb[:, :, n, :], U.rearrange("(a p) h -> p a h", p=P)).then_inc(weights_in, 16)
                act.dma_start(V_sb[:, :, n, :], V.rearrange("(a p) h -> p a h", p=P)).then_inc(weights_in, 16)
                with nc.allow_non_contiguous_dma("bias columns"):
                    act.dma_start(gb[:, n, :], b.rearrange("(a p) -> p a", p=P)).then_inc(weights_in, 16)

            sqrts = [0]

            def deviation(j0, j1):
                sqrts[0] += 1
                act.wait_ge(var_ready, sqrts[0])
                nc.scalar.activation(sd[:, j0:j1], var_eps[:, j0:j1], ACT.Sqrt).then_inc(sqrt_ready, 1)

            deviation(0, X_CHUNK)
            for c in range(BLOCKS // X_CHUNK):
                if (c + 1) * X_CHUNK < BLOCKS:
                    deviation((c + 1) * X_CHUNK, (c + 2) * X_CHUNK)
                for j in range(c * X_CHUNK, (c + 1) * X_CHUNK + (2 if (c + 1) * X_CHUNK == BLOCKS else 0)):
                    if j == 0:
                        act.wait_ge(scales_ready, 1)
                        nc.scalar.activation(W16[:, 0, :, :], w_sb, ACT.Copy, scale=w_scale[:, 0:1]
                                             ).then_inc(w_hi, 1)
                    if j < BLOCKS:
                        act.wait_ge(zT_ps, j + 1)
                        if j >= 3:
                            act.wait_ge(line_ps, j - 2)
                        nc.scalar.activation(zT[:, j % 3, 0, :, :],
                                             bank[5 + j % 2][:, 0:DH * NB].rearrange("p (d n) -> p d n", d=DH),
                                             ACT.Copy).then_inc(zT_hi, 1)
                    if j >= 2:
                        act.wait_ge(line_ps, j - 1)
                        nc.scalar.activation(line[:, j - 2, D:2 * D], bank[(j - 2) % 2][0:NB, 0:D], ACT.Copy
                                             ).then_inc(line_hi, 1)

            for n in range(3):
                for u, (w, w16) in enumerate(((U_sb, U16), (V_sb, V16))):
                    if n + u == 0:
                        act.wait_ge(weights_in, 16 * 9)
                    nc.scalar.activation(w16[:, 0, :, n * H:(n + 1) * H], w[:, :, n, :], ACT.Copy,
                                         scale=w_scale[:, 1 + u:2 + u]).then_inc(uv_hi, 1)

            tile = 0

            def gates_out(j0, j1, tiles=range(MT)):
                nonlocal tile
                for m in tiles:
                    act.wait_ge(gx_ps, tile + 1)
                    nc.scalar.activation(gx[:, :, m, j0 * CPB:j1 * CPB],
                                         ps_gates[tile % 2][:, 0:(j1 - j0) * NB].rearrange("p (k s) -> p s k",
                                                                                           s=STEPS),
                                         ACT.Identity, bias=gb[:, m // HH, m % HH:m % HH + 1],
                                         scale=w_unscale[:, 1:2]).then_inc(gx_ready, 1)
                    tile += 1

            for j in range(BLOCKS + LAG):
                for i in range(WINDOWS):
                    w = j * WINDOWS + i
                    if j < BLOCKS:
                        act.wait_ge(count_ps, w + 1)
                        if i == 0 and j >= 2:
                            act.wait_ge(sum_ps, j - 1)
                        n0 = NB * i // WINDOWS
                        n = SPAN[w]
                        nc.scalar.activation(counts[:, j % 2, :, n0:n0 + n],
                                             ps_count[w % 3][0:NB, 0:n * BLOCKS].rearrange("p (n s) -> p s n", n=n),
                                             ACT.Copy).then_inc(counted, 1)
                    for _, (j0, j1), m in gates_at(j, i - 1):
                        gates_out(j0, j1, [m])
                    t = j - ROOT_AT[1]
                    if i == ROOT_AT[0] and 0 <= t < BLOCKS:
                        deviation(t, t + 1)
                    t = j - HIGH_AT[1]
                    if i == HIGH_AT[0] and 0 <= t < BLOCKS:
                        act.wait_ge(z2T_ps, t + 1)
                        if t >= 2 * TB and t % TB == 0:
                            act.wait_ge(gx_ps, MT * (t // TB - 1))
                        nc.scalar.activation(z2T[:, (t // TB) % 2, 0, :, t % TB, :],
                                             ps_zT[:, 0:DH * NB].rearrange("p (d n) -> p d n", d=DH),
                                             ACT.Copy).then_inc(z2T_hi, 1)

            def general_block(j):
                deviation(j, j + 1)
                act.wait_ge(z2T_ps, BLOCKS + j + 1)
                nc.scalar.activation(z2T[:, 0, 0, :, 0, :],
                                     ps_zT[:, 0:DH * NB].rearrange("p (d n) -> p d n", d=DH),
                                     ACT.Copy).then_inc(z2T_hi, 1)
                gates_out(j, j + 1)

            where_open(act, general_block)

            def run_round(first, done, starts):
                def step(s, turn):
                    for q, (c0, c1) in enumerate(COLS):
                        n = c1 - c0
                        act.wait_ge(ig_pre[q], turn)
                        nc.scalar.activation(gate[:, q, 0:2 * HH, 0:n], pre[:, q, 0:2 * HH, 0:n], ACT.Tanh
                                             ).then_inc(ig_gate[q], 1)
                        act.wait_ge(o_pre[q], turn)
                        nc.scalar.activation(gate[:, q, 2 * HH:MT, 0:n], pre[:, q, 2 * HH:MT, 0:n], ACT.Tanh
                                             ).then_inc(o_gate[q], 1)
                        act.wait_ge(c_ready[q], turn)
                        nc.scalar.activation(tc[:, q, :, 0:n], c_all[:, bass.ds(s + 1, 1), :, c0:c1], ACT.Tanh,
                                             scale=0.5).then_inc(tc_ready[q], 1)

                step(first, done + 1)
                for s in steps_of(act, first, done):
                    for u in range(UNROLL):
                        step(s + u, s + (done - first + 1 + u))

            at_each_round(act, run_round)

            for j in range(BLOCKS):
                if j >= 3:
                    act.wait_ge(hT_ready, j - 2)
                nc.scalar.activation(h_out[:, j % 3, :, :].rearrange("p m (k s) -> p m k s", s=STEPS),
                                     h_all[:, 1:STEPS + 1, :, j * CPB:(j + 1) * CPB].rearrange("p s m k -> p m k s"),
                                     ACT.Copy).then_inc(h_out_ready, 1)

        @block.tensor
        def _(pe):
            pe.wait_ge(consts, 5)
            pe.wait_ge(before_ready, 1)
            for b in range(WIN_BATCHES):
                mm = nc.tensor.matmul(bank[7][0:WIN_ROWS, b:b + 1], before[:, b * WIN_ROWS:(b + 1) * WIN_ROWS],
                                      ones[0:EDGE_ROWS, 0:1], start=True, stop=True)
            mm.then_inc(before_ps, 1)

            for j in range(BLOCKS + 2):
                if j < BLOCKS:
                    pe.wait_ge(z_ready, j + 1)
                    if j >= 2:
                        pe.wait_ge(zT_ready, j - 1)
                    for d in range(DH):
                        mm = nc.tensor.transpose(bank[5 + j % 2][:, d * NB:(d + 1) * NB],
                                                 z[:, j % 3, d * P:(d + 1) * P], ident[0:NB, 0:NB])
                    mm.then_inc(zT_ps, 1)
                if j >= 2:
                    t = j - 2
                    pe.wait_ge(zT_ready, t + 1)
                    if t == 0:
                        pe.wait_ge(w_split, 1)
                    if t >= 2:
                        pe.wait_ge(line_ready, t - 1)
                    parts = [(d, w_part, z_part) for w_part, z_part in PRODUCTS for d in range(DH)]
                    for n, (d, w_part, z_part) in enumerate(parts):
                        mm = nc.tensor.matmul(bank[t % 2][0:NB, 0:D], zT[:, t % 3, z_part, d, :],
                                              W16[:, w_part, d, :], start=(n == 0), stop=(n == len(parts) - 1))
                    mm.then_inc(line_ps, 1)

            pe.wait_ge(edges_f, 1)
            for a in range(2):
                for t in range(WIN_TILES):
                    for b in range(WIN_BATCHES):
                        mm = nc.tensor.transpose(bank[2 + 2 * a + t][:, b * WIN_ROWS:(b + 1) * WIN_ROWS],
                                                 win_edges_f[:, a, b, t * P:(t + 1) * P],
                                                 ident[0:WIN_ROWS, 0:WIN_ROWS])
            mm.then_inc(edges_ps, 1)

            def sums(j, s):
                nc.tensor.matmul(ps_sum[j % 2][:, 0:D + 1], counts[:, j % 2, s, :], line[:, s, D:2 * D + 1],
                                 start=(s == 0), stop=False, skip_group_check=True)
                return nc.tensor.matmul(ps_sum[j % 2][:, 0:D], counts[:, j % 2, s, :], line[:, s, 0:D],
                                        start=False, stop=(s == BLOCKS - 1), skip_group_check=True)

            def turn_z2(t):
                pe.wait_ge(z2_ready, t + 1)
                if t >= 1:
                    pe.wait_ge(z2T_ready, t)
                for d in range(DH):
                    mm = nc.tensor.transpose(ps_zT[:, d * NB:(d + 1) * NB], z2[:, t % 2, d * P:(d + 1) * P],
                                             ident[0:NB, 0:NB])
                mm.then_inc(z2T_ps, 1)

            tile = 0

            def gates_x(n_blocks, buf, turned, tiles=range(MT)):
                nonlocal tile
                pe.wait_ge(z2T_ready, turned)
                if tile == 0:
                    pe.wait_ge(uv_split, 6)
                for m in tiles:
                    if tile >= 2:
                        pe.wait_ge(gx_ready, tile - 1)
                    parts = [(d, w_part, z_part) for w_part, z_part in PRODUCTS for d in range(DH)]
                    for n, (d, w_part, z_part) in enumerate(parts):
                        mm = nc.tensor.matmul(ps_gates[tile % 2][:, 0:n_blocks * NB],
                                              U16[:, w_part, d, m * P:(m + 1) * P],
                                              z2T[:, buf, z_part, d, 0:n_blocks, :].rearrange("p s k -> p (s k)"),
                                              start=(n == 0), stop=(n == len(parts) - 1))
                    mm.then_inc(gx_ps, 1)
                    tile += 1

            pe.wait_ge(keys_ready, 1)
            pe.wait_ge(line_ready, BLOCKS)
            pooled = 0
            for j in range(BLOCKS + LAG):
                for i in range(WINDOWS):
                    w = j * WINDOWS + i
                    if j < BLOCKS:
                        pe.wait_ge(hot_ready, w + 1)
                        if on_pool(w):
                            pooled += 1
                            pe.wait_ge(hot_p_pool, pooled)
                        if w >= 3:
                            pe.wait_ge(counted, w - 2)
                        n = SPAN[w] * BLOCKS
                        for t in range(WIN_TILES):
                            mm = nc.tensor.matmul(ps_count[w % 3][:, 0:n], hot_p[:, w % HOTS, t, :],
                                                  hot_ts[:, w % HOTS, t, 0:n], start=(t == 0),
                                                  stop=(t == WIN_TILES - 1))
                        mm.then_inc(count_ps, 1)
                    for b, (j0, j1), m in gates_at(j, i):
                        gates_x(j1 - j0, b % 2, j1, [m])
                    if 1 <= j <= BLOCKS:
                        if i == 0:
                            pe.wait_ge(counted, j * WINDOWS)
                            if j >= 3:
                                pe.wait_ge(x1_ready, j - 2)
                        for s in range(BLOCKS * i // WINDOWS, BLOCKS * (i + 1) // WINDOWS):
                            mm = sums(j - 1, s)
                        if i == WINDOWS - 1:
                            mm.then_inc(sum_ps, 1)
                    if i == TURN_AT[0] and 0 <= j - TURN_AT[1] < BLOCKS:
                        turn_z2(j - TURN_AT[1])
            pe.wait_ge(covered_ready, 1)
            nc.tensor.matmul(ps_t[0][0:1, 0:1], covered[:, :], ones[:, 0:1], start=True, stop=True
                             ).then_inc(covered_ps, 1)

            def general_block(j):
                turn_block = BLOCKS + j
                bank_sum = ps_sum[turn_block % 2]
                pe.wait_ge(x1_ready, turn_block - 1)
                run = j // G_RUN * G_RUN

                def one(e, b):
                    turn = e + j * EDGE_COLS
                    pe.wait_ge(g_hot_ready, turn + 1)
                    per_block = EDGE_COLS // 2 + 1 - b
                    if isinstance(e, int):
                        pe.wait_ge(g_rows_in[j // G_RUN][b], 16 * ((j - run) * per_block + e // 2 + 1))
                    else:
                        pe.wait_ge(g_rows_in[j // G_RUN][b], e * 8 + (16 * (j - run) * per_block + 8 * (2 - b)))
                    first, last = (isinstance(e, int) and e == v for v in (0, EDGE_COLS - 1))
                    nc.tensor.matmul(bank_sum[:, 0:D + 1], g_hot[:, b, :], g_rows[:, b, D:2 * D + 1],
                                     start=first, stop=False, skip_group_check=True)
                    nc.tensor.matmul(bank_sum[:, 0:D], g_hot[:, b, :], g_rows[:, b, 0:D],
                                     start=False, stop=last, skip_group_check=True).then_inc(g_used, 1)
                tiles_of(pe, one)
                pe.wait_ge(g_used, (j + 1) * EDGE_COLS)
                nc.tensor.matmul(ps_t[0][0:1, 0:1], covered[:, :], ones[:, 0:1], start=True, stop=True
                                 ).then_inc(sum_ps, 1)
                turn_z2(turn_block)
                gates_x(1, 0, turn_block + 1)

            where_open(pe, general_block)

            def run_round(first, done, starts):
                def step(seen, turn):
                    for q, (c0, c1) in enumerate(COLS):
                        n = c1 - c0
                        pe.wait_ge(hi_ready[q], seen)
                        for to, m0, m1, done_sem in ((ps_g[q], 0, 2 * HH, ig_ps[q]), (ps_x[q], 2 * HH, MT, o_ps[q])):
                            for v_part, h_part in PRODUCTS:
                                if h_part == 1 and m0 == 0:
                                    pe.wait_ge(lo_ready[q], seen if q == 0 else turn)
                                for m in range(m0, m1):
                                    for d in range(HH):
                                        mm = nc.tensor.matmul(
                                            to[:, (m - m0) * n:(m - m0 + 1) * n], V16[:, v_part, d, m * P:(m + 1) * P],
                                            h16[:, h_part, d, c0:c1],
                                            start=(v_part + h_part + d == 0 and m == m0),
                                            stop=(h_part == 1 and d == HH - 1), skip_group_check=True)
                            mm.then_inc(done_sem, 1)

                step(done + starts, done + 1)
                for s in steps_of(pe, first, done):
                    for u in range(UNROLL):
                        step(s + (done - first + starts + u), s + (done - first + 1 + u))

            def count_near():
                pe.wait_ge(near_ready, 1)
                nc.tensor.matmul(ps_t[0][0:1, 0:1], near[:, :], ones[:, 0:1], start=True, stop=True
                                 ).then_inc(near_ps, 1)

            at_each_round(pe, run_round, count_near)

            for j in range(BLOCKS):
                pe.wait_ge(h_out_ready, j + 1)
                if j >= 2:
                    pe.wait_ge(out_ready, j - 1)
                for d in range(HH):
                    mm = nc.tensor.transpose(ps_t[j % 2][0:NB, d * P:(d + 1) * P], h_out[:, j % 3, d, :],
                                             ident[:, :])
                mm.then_inc(hT_ready, 1)

        @block.vector
        def _(dve):
            seq = [0]

            def flat(w):
                return w[:, :, :, :].rearrange("p d n h -> p (d n h)")

            linked = [dve_seq]

            def link(ins):
                seq[0] += 1
                ins.then_inc(linked[0], 1)
                dve.wait_ge(linked[0], seq[0])

            def norm_stats(s, t):
                link(nc.vector.bn_stats(stats[:, s, :], t))
                nc.vector.bn_aggr(mv[:, s, :], stats[:, s, :]).then_inc(linked[0], 1)
                seq[0] += 1

            sqrts = [0]

            def to_root(j0, j1):
                nc.vector.tensor_scalar(var_eps[:, j0:j1], mv[:, j0:j1, 1], EPS, None, ALU.add
                                        ).then_inc(var_ready, 1)

            def inverse_deviation(j0, j1):
                ve, y, t = var_eps[:, j0:j1], rstd[:, j0:j1], newton[:, j0:j1]
                sqrts[0] += 1
                dve.wait_ge(sqrt_ready, sqrts[0])
                link(nc.vector.reciprocal(y, sd[:, j0:j1]))
                link(nc.vector.tensor_tensor(t, y, y, ALU.mult))
                link(nc.vector.tensor_tensor(t, t, ve, ALU.mult))
                link(nc.vector.tensor_scalar(t, t, -0.5, 1.5, ALU.mult, ALU.add))
                link(nc.vector.tensor_tensor(y, y, t, ALU.mult))

            def whole_part(t, scale, shift):
                link(nc.vector.tensor_scalar(t, t, scale, shift, ALU.mult, ALU.add))
                link(nc.vector.tensor_scalar(t, t, ROUND, None, ALU.add))
                link(nc.vector.tensor_scalar(t, t, ROUND, None, ALU.subtract))

            dve.wait_ge(iotas, 2)
            for t in (row_thr, col_thr):
                whole_part(t, NB / WINDOWS, -(WINDOWS - 1) / (2.0 * WINDOWS))
            dve.wait_ge(dst_rows_in, 16)
            link(nc.vector.tensor_copy(first_row, dst_rows[:, 0:1]))
            nc.vector.tensor_scalar(before, row_thr[0:EDGE_ROWS, 0:NWP], first_row, None, ALU.is_gt
                                    ).then_inc(before_ready, 1)
            link(nc.vector.tensor_tensor(limit, row_thr[:, 1:NWP + 1], row_thr[:, 0:NWP], ALU.subtract))
            link(nc.vector.tensor_scalar(limit, limit, float(BLOCKS), None, ALU.mult))
            dve.wait_ge(before_ps, 1)
            link(nc.vector.tensor_scalar(row_f, bank[7][0:WIN_ROWS, 0:WIN_BATCHES], 1.0, 0.0, ALU.subtract, ALU.max))
            nc.vector.tensor_copy(row_i, row_f).then_inc(rows_known, 1)

            dve.wait_ge(w_in, 16)
            dve.wait_ge(weights_in, 16 * 9)
            for n, w in enumerate((w_sb.rearrange("p d h -> p (d h)"), flat(U_sb), flat(V_sb))):
                link(nc.vector.tensor_reduce(w_max[:, n:n + 1], w, AX_X, ALU.max))
                link(nc.vector.tensor_reduce(w_min[:, n:n + 1], w, AX_X, ALU.min))
            link(nc.vector.scalar_tensor_tensor(out=w_max[:, :], in0=w_min[:, :], scalar=-1.0, in1=w_max[:, :],
                                                op0=ALU.mult, op1=ALU.max))
            nc.vector.tensor_scalar(w_max[:, :], w_max[:, :], 2.0 ** -100, None, ALU.max).then_inc(w_max_ready, 1)

            def norm_chunk(c):
                dve.wait_ge(x_in[c], 16)
                for j in range(c * X_CHUNK, (c + 1) * X_CHUNK):
                    norm_stats(j, x_sb[:, j, :])
                dve.wait_ge(dve_seq, seq[0])
                to_root(c * X_CHUNK, (c + 1) * X_CHUNK)

            norm_chunk(0)
            dve.wait_ge(w_max_all, 1)
            link(nc.vector.tensor_scalar(w_exp[:, :], w_top[:, :].bitcast(I32), 0x7F800000, None, ALU.bitwise_and))
            for n0, n1, top in ((0, 1, 6), (1, 3, 13)):
                link(nc.vector.tensor_scalar(w_scale[:, n0:n1].bitcast(I32), w_exp[:, n0:n1], -1.0,
                                             float((127 + 127 + top) << 23), ALU.mult, ALU.add))
                link(nc.vector.tensor_scalar(w_unscale[:, n0:n1].bitcast(I32), w_exp[:, n0:n1], -float(top << 23), None,
                                             ALU.add))
            for n, half in ((0, 0.5), (2, 0.5)):
                nc.vector.tensor_scalar(U_sb[:, :, n, :], U_sb[:, :, n, :], half, None, ALU.mult
                                        ).then_inc(dve_seq, 1)
                nc.vector.tensor_scalar(gb[:, n, :], gb[:, n, :], half, None, ALU.mult).then_inc(dve_seq, 1)
                nc.vector.tensor_scalar(V_sb[:, :, n, :], V_sb[:, :, n, :], half * 0.5, None, ALU.mult
                                        ).then_inc(dve_seq, 1)
                seq[0] += 3
            link(nc.vector.tensor_scalar(V_sb[:, :, 1, :], V_sb[:, :, 1, :], 0.5, None, ALU.mult))
            nc.vector.memset(far_f[:, :], 0.0).then_inc(scales_ready, 1)

            def window_starts():
                for b in range(WIN_BATCHES):
                    dve.wait_ge(win_rows_in[b], 16)
                link(nc.vector.tensor_copy(win_rows_f, win_rows))
                for b in range(WIN_BATCHES):
                    link(nc.vector.tensor_scalar(win_rows_f[:, b, :], win_rows_f[:, b, :], col_thr[:, b:b + 1], None,
                                                 ALU.is_lt))
                link(nc.vector.tensor_reduce(in_row, win_rows_f, AX_X, ALU.add))
                link(nc.vector.scalar_tensor_tensor(out=start_f, in0=row_f, scalar=float(EDGE_COLS), in1=in_row,
                                                    op0=ALU.mult, op1=ALU.add))
                link(nc.vector.tensor_scalar(start_f, start_f, float(E - WIN_EDGES), None, ALU.min))
                nc.vector.tensor_copy(start_i, start_f).then_inc(starts_known, 1)

            def window_edges():
                for sems in win_edges_in:
                    for s in sems:
                        dve.wait_ge(s, 16)
                nc.vector.tensor_copy(win_edges_f, win_edges).then_inc(edges_f, 1)

            for c in range(BLOCKS // X_CHUNK):
                if (c + 1) * X_CHUNK < BLOCKS:
                    norm_chunk(c + 1)
                inverse_deviation(c * X_CHUNK, (c + 1) * X_CHUNK)
                for j in range(c * X_CHUNK, (c + 1) * X_CHUNK + (4 if (c + 1) * X_CHUNK == BLOCKS else 0)):
                    if j < BLOCKS:
                        if j >= 3:
                            dve.wait_ge(zT_ps, j - 2)
                        nc.vector.tensor_scalar(z[:, j % 3, :], x_sb[:, j, :], mv[:, j, 0:1], rstd[:, j:j + 1],
                                                ALU.subtract, ALU.mult).then_inc(z_ready, 1)
                    if j == 1:
                        dve.wait_ge(w_hi, 1)
                        nc.vector.scalar_tensor_tensor(out=W16[:, 1, :, :], in0=w_sb, scalar=w_scale[:, 0:1],
                                                       in1=W16[:, 0, :, :], op0=ALU.mult, op1=ALU.subtract
                                                       ).then_inc(w_split, 1)
                        window_starts()
                    if j >= 2 and j - 2 < BLOCKS:
                        t = j - 2
                        dve.wait_ge(zT_hi, t + 1)
                        nc.vector.tensor_tensor(zT[:, t % 3, 1, :, :],
                                                bank[5 + t % 2][:, 0:DH * NB].rearrange("p (d n) -> p d n", d=DH),
                                                zT[:, t % 3, 0, :, :], ALU.subtract).then_inc(zT_ready, 1)
                    if j >= 4:
                        t = j - 4
                        dve.wait_ge(line_hi, t + 1)
                        nc.vector.tensor_tensor(line[:, t, 0:D], bank[t % 2][0:NB, 0:D], line[:, t, D:2 * D],
                                                ALU.subtract).then_inc(line_ready, 1)
                if c == 2:
                    window_edges()

            dve.wait_ge(edges_ps, 1)
            for t in range(WIN_TILES):
                nc.vector.tensor_tensor(rel[:, t, :], bank[2 + t][:, 0:NWP], row_thr[:, 0:NWP], ALU.subtract
                                        ).then_inc(dve_seq, 1)
                link(nc.vector.tensor_scalar(slot[:, t, :], bank[4 + t][:, 0:NWP], 1.0 / NB, -(NB - 1) / (2.0 * NB),
                                             ALU.mult, ALU.add))
                seq[0] += 1
            dve.wait_ge(dve_seq, seq[0])
            link(nc.vector.tensor_scalar(slot, slot, ROUND, None, ALU.add))
            link(nc.vector.tensor_scalar(slot, slot, ROUND, None, ALU.subtract))
            for t in range(WIN_TILES):
                link(nc.vector.scalar_tensor_tensor(out=part[:, t, :], in0=slot[:, t, :], scalar=-float(NB),
                                                    in1=bank[4 + t][:, 0:NWP], op0=ALU.mult, op1=ALU.add))
            link(nc.vector.scalar_tensor_tensor(out=key[:, :, :], in0=rel, scalar=float(BLOCKS), in1=slot,
                                                op0=ALU.mult, op1=ALU.add))
            nc.vector.memset(far_f[:, :], 0.0).then_inc(keys_ready, 1)
            dve.wait_ge(consts, 5)

            def finish(j, turn):
                if j == 0:
                    dve.wait_ge(b_in, 16)
                dve.wait_ge(sum_ps, turn + 1)
                number = ps_sum[turn % 2][0:NB, D:D + 1]
                nc.vector.tensor_scalar(has[:, :], number, 1.0, None, ALU.min).then_inc(linked[0], 1)
                seq[0] += 1
                link(nc.vector.tensor_scalar(inv[:, :], number, 1.0, None, ALU.max))
                link(nc.vector.reciprocal(inv[:, :], inv[:, :]))
                link(nc.vector.tensor_tensor(inv[:, :], inv[:, :], w_unscale[0:NB, 0:1], ALU.mult))
                link(nc.vector.scalar_tensor_tensor(out=x_sb[:, j, :], in0=b_bc[:, :], scalar=has[:, 0:1],
                                                    in1=x_sb[:, j, :], op0=ALU.mult, op1=ALU.add))
                nc.vector.scalar_tensor_tensor(out=x_sb[:, j, :], in0=ps_sum[turn % 2][0:NB, 0:D], scalar=inv[:, 0:1],
                                               in1=x_sb[:, j, :], op0=ALU.mult, op1=ALU.add).then_inc(x1_ready, 1)
                dve.wait_ge(x1_ready, turn + 1)
                norm_stats(j, x_sb[:, j, :])
                dve.wait_ge(linked[0], seq[0])
                to_root(j, j + 1)

            def second_norm(j, turn):
                inverse_deviation(j, j + 1)
                if turn >= 2:
                    dve.wait_ge(z2T_ps, turn - 1)
                nc.vector.tensor_scalar(z2[:, turn % 2, :], x_sb[:, j, :], mv[:, j, 0:1], rstd[:, j:j + 1],
                                        ALU.subtract, ALU.mult).then_inc(z2_ready, 1)

            def second_low(turn, buf, pos):
                dve.wait_ge(z2T_hi, turn + 1)
                nc.vector.tensor_tensor(z2T[:, buf, 1, :, pos, :],
                                        ps_zT[:, 0:DH * NB].rearrange("p (d n) -> p d n", d=DH),
                                        z2T[:, buf, 0, :, pos, :], ALU.subtract).then_inc(z2T_ready, 1)

            for j in range(BLOCKS + LAG):
                for i in range(WINDOWS):
                    w = j * WINDOWS + i
                    if j < BLOCKS:
                        if w >= HOTS:
                            dve.wait_ge(count_ps, w - HOTS + 1)
                        for t in range(WIN_TILES):
                            if not on_pool(w):
                                nc.vector.tensor_scalar(hot_p[:, w % HOTS, t, :], iota[:, 0:P], part[:, t, w:w + 1],
                                                        None, ALU.is_equal).then_inc(dve_seq, 1)
                                seq[0] += 1
                            n = SPAN[w] * BLOCKS
                            ins = nc.vector.tensor_scalar(hot_ts[:, w % HOTS, t, 0:n], iota[:, 0:n],
                                                          key[:, t, w:w + 1], None, ALU.is_equal)
                        ins.then_inc(hot_ready, 1)
                    for at_i, behind in (FINISH_AT, NORM_AT, LOW_AT):
                        b = j - behind
                        if i != at_i or not 0 <= b < BLOCKS:
                            continue
                        if (at_i, behind) == FINISH_AT:
                            finish(b, b)
                        elif (at_i, behind) == NORM_AT:
                            second_norm(b, b)
                        else:
                            second_low(b, b // TB % 2, b % TB)
                if j < 6:
                    dve.wait_ge(uv_hi, j + 1)
                    n, (u, w, w16) = j // 2, ((1, U_sb, U16), (2, V_sb, V16))[j % 2]
                    nc.vector.scalar_tensor_tensor(out=w16[:, 1, :, n * H:(n + 1) * H], in0=w[:, :, n, :],
                                                   scalar=w_scale[:, u:u + 1], in1=w16[:, 0, :, n * H:(n + 1) * H],
                                                   op0=ALU.mult, op1=ALU.subtract).then_inc(uv_split, 1)
                if j == 6:
                    wide = limit.unsqueeze(1).to_broadcast([P, WIN_TILES, NWP])
                    link(nc.vector.tensor_scalar(inside, key[:, :, :], 0.0, None, ALU.is_ge))
                    link(nc.vector.tensor_tensor(rel, key[:, :, :], wide, ALU.is_lt))
                    link(nc.vector.tensor_tensor(inside, inside, rel, ALU.mult))
                    nc.vector.tensor_reduce(covered[:, :], inside.rearrange("p t w -> p (t w)"), AX_X, ALU.add
                                            ).then_inc(covered_ready, 1)
            dve.wait_ge(covered_ps, 1)
            link(nc.vector.tensor_scalar(open_f[:, :], ps_t[0][0:1, 0:1], float(E), None, ALU.not_equal))
            nc.vector.tensor_copy(open_i[:, :], open_f[:, :]).then_inc(open_ready, 1)

            chain = seq[0]
            linked[0], seq[0] = g_seq, 0

            def general_start():
                dve.wait_ge(g_in, 48)
                link(nc.vector.tensor_copy(g_dst_f, g_dst))

            def general_block(j):
                link(nc.vector.tensor_scalar(g_rel, g_dst_f, -float(j * NB), None, ALU.add))

                def one(e, b):
                    turn = e + j * EDGE_COLS
                    if not isinstance(e, int) or turn >= 2:
                        dve.wait_ge(g_used, turn - (0 if isinstance(e, int) and e == 0 else 1))
                        dve.sem_inc(waits_passed)
                    nc.vector.tensor_scalar(g_hot[:, b, :], iota[0:EDGE_ROWS, 0:P], g_rel[:, bass.ds(e, 1)], None,
                                            ALU.is_equal).then_inc(g_hot_ready, 1)
                tiles_of(dve, one)
                turn = BLOCKS + j
                finish(j, turn)
                second_norm(j, turn)
                second_low(turn, 0, 0)
                dve.wait_ge(gx_ready, MT * (len(BATCHES) + j + 1))

            where_open(dve, general_block, general_start)
            linked[0], seq[0] = dve_seq, chain

            dve.wait_ge(gx_ready, MT * len(BATCHES))
            nc.vector.memset(h_all[:, 0, :, 0:1], 0.0).then_inc(start_set, 1)
            nc.vector.memset(c_all[:, 0, :, 0:1], 0.0).then_inc(start_set, 1)
            dve.wait_ge(start_set, 2)

            def run_round(first, done, starts):
                if first == 0:
                    for q in range(2):
                        dve.wait_ge(h_ready[q], done + starts - 1)
                    dve.wait_ge(lo_ready[0], done + starts - 1)
                for q, (c0, c1) in enumerate(COLS):
                    if first == 0:
                        k0 = max(c0, 1)
                        nc.vector.tensor_copy(h_all[:, 0, :, k0:c1], h_all[:, STEPS, :, k0 - 1:c1 - 1]
                                              ).then_inc(h_ready[q], 1)
                    else:
                        nc.vector.memset(h_all[:, first, :, c0:c1], 0.0).then_inc(h_ready[q], 1)
                if first == 0:
                    nc.vector.tensor_copy(c_all[:, 0, :, 1:CHUNKS], c_all[:, STEPS, :, 0:CHUNKS - 1]
                                          ).then_inc(start_ready, 1)
                else:
                    nc.vector.memset(c_all[:, first, :, :], 0.0).then_inc(start_ready, 1)
                for q, (c0, c1) in enumerate(COLS):
                    dve.wait_ge(h_ready[q], done + starts)
                    nc.vector.tensor_scalar(h16[:, 0, :, c0:c1], h_all[:, first, :, c0:c1], 1.0, None, ALU.mult
                                            ).then_inc(hi_ready[q], 1)
                dve.wait_ge(start_ready, starts)
                dve.sem_inc(waits_passed)

                def ops(q, s, turn):
                    c0, c1 = COLS[q]
                    n = c1 - c0
                    now, then = bass.ds(s, 1), bass.ds(s + 1, 1)
                    v_ig = ps_g[q][:, 0:2 * HH * n].rearrange("p (m k) -> p m k", k=n)
                    v_o = ps_x[q][:, 0:HH * n].rearrange("p (m k) -> p m k", k=n)

                    def arg_ig():
                        dve.wait_ge(ig_ps[q], turn)
                        nc.vector.scalar_tensor_tensor(out=pre[:, q, 0:2 * HH, 0:n], in0=v_ig,
                                                       scalar=w_unscale[:, 2:3], in1=gx[:, now, 0:2 * HH, c0:c1],
                                                       op0=ALU.mult, op1=ALU.add).then_inc(ig_pre[q], 1)

                    def arg_o():
                        dve.wait_ge(o_ps[q], turn)
                        nc.vector.scalar_tensor_tensor(out=pre[:, q, 2 * HH:MT, 0:n], in0=v_o,
                                                       scalar=w_unscale[:, 2:3], in1=gx[:, now, 2 * HH:MT, c0:c1],
                                                       op0=ALU.mult, op1=ALU.add).then_inc(o_pre[q], 1)

                    def new_part():
                        dve.wait_ge(ig_gate[q], turn)
                        nc.vector.scalar_tensor_tensor(out=ig[:, q, :, 0:n], in0=gate[:, q, 0:HH, 0:n], scalar=1.0,
                                                       in1=gate[:, q, HH:2 * HH, 0:n], op0=ALU.add, op1=ALU.mult
                                                       ).then_inc(ig_ready[q], 1)

                    def cell():
                        dve.wait_ge(hc_ready[q], turn)
                        dve.wait_ge(ig_ready[q], turn)
                        nc.vector.scalar_tensor_tensor(out=c_all[:, then, :, c0:c1], in0=hc[:, q, :, 0:n], scalar=0.5,
                                                       in1=ig[:, q, :, 0:n], op0=ALU.mult, op1=ALU.add
                                                       ).then_inc(c_ready[q], 1)

                    def state():
                        dve.wait_ge(tc_ready[q], turn)
                        for h_out, ready in ((h16[:, 0, :, c0:c1], hi_ready[q]), (h_all[:, then, :, c0:c1], h_ready[q])):
                            nc.vector.scalar_tensor_tensor(out=h_out, in0=gate[:, q, 2 * HH:MT, 0:n], scalar=1.0,
                                                           in1=tc[:, q, :, 0:n], op0=ALU.add, op1=ALU.mult
                                                           ).then_inc(ready, 1)

                    return arg_ig, arg_o, new_part, cell, state

                def both(s, turn, before):
                    a_arg_ig, a_arg_o, a_new, a_cell, a_state = ops(0, s, turn)
                    b_arg_ig, b_arg_o, b_new, b_cell, b_state = ops(1, s, turn)
                    a_arg_ig()
                    if before:
                        ops(1, s - 1, turn - 1)[4]()
                    a_arg_o()
                    a_new()
                    a_cell()
                    b_arg_ig()
                    a_state()
                    b_arg_o()
                    b_new()
                    b_cell()

                both(first, done + 1, False)
                for s in steps_of(dve, first, done):
                    for u in range(UNROLL):
                        both(s + u, s + (done - first + 1 + u), True)
                ops(1, STEPS - 1, done + STEPS - first)[4]()

            def count_near():
                for q in range(2):
                    dve.wait_ge(h_ready[q], DONE + len(ROUNDS))
                for n, state in enumerate((h_all, c_all)):
                    link(nc.vector.tensor_tensor(gap[:, n, :, :], state[:, STEPS, :, 0:CHUNKS - 1],
                                                 state[:, 0, :, 1:CHUNKS], ALU.subtract))
                link(nc.vector.tensor_tensor(gap[:, :, :, :], gap[:, :, :, :], gap[:, :, :, :], ALU.mult))
                link(nc.vector.tensor_scalar(gap[:, :, :, :], gap[:, :, :, :], STATE_TOL ** 2, None, ALU.is_le))
                nc.vector.tensor_reduce(near[:, :], gap[:, :, :, :].rearrange("p a m k -> p (a m k)"), AX_X, ALU.add
                                        ).then_inc(near_ready, 1)
                dve.wait_ge(near_ps, 1)
                link(nc.vector.tensor_scalar(far_f[:, :], ps_t[0][0:1, 0:1], float(P * 2 * HH * (CHUNKS - 1)), None,
                                             ALU.is_lt))
                nc.vector.tensor_copy(far_i[:, :], far_f[:, :]).then_inc(far_ready, 1)

            at_each_round(dve, run_round, count_near)

            for j in range(BLOCKS):
                dve.wait_ge(hT_ready, j + 1)
                nc.vector.scalar_tensor_tensor(out=x_sb[:, j, :], in0=ps_t[j % 2][0:NB, 0:H], scalar=0.5,
                                               in1=x_sb[:, j, :], op0=ALU.mult, op1=ALU.add).then_inc(out_ready, 1)


_INS = ['x', 'src', 'dst', 'L0_gnn_weight', 'L0_gnn_bias', 'L0_ffn_U_i', 'L0_ffn_V_i', 'L0_ffn_b_i',
        'L0_ffn_U_c', 'L0_ffn_V_c', 'L0_ffn_b_c', 'L0_ffn_U_o', 'L0_ffn_V_o', 'L0_ffn_b_o']


def kernel(**inputs):
    import numpy as _np
    import concourse.bacc as _bacc
    from concourse import mybir as _mybir
    from concourse.bass_utils import run_bass_kernel_spmd as _run

    nc = _bacc.Bacc("TRN2", target_bir_lowering=False, num_devices=1)
    arrays, args = {}, []
    for name in _INS:
        a = _np.ascontiguousarray(inputs[name])
        arrays[f"in_{name}_dram"] = a
        args.append(nc.dram_tensor(f"in_{name}_dram", a.shape, _mybir.dt.from_np(a.dtype), kind="ExternalInput").ap())
    args.append(nc.dram_tensor("out_0_dram", inputs["x"].shape, _mybir.dt.float32, kind="ExternalOutput").ap())
    bass_gnn_lstm_kernel(nc, *args)
    r = _run(nc, [arrays], core_ids=[0])
    return r.results[0]["out_0_dram"]
```

```python
from contextlib import ExitStack

import concourse.bass as bass
from concourse import mybir

F32 = mybir.dt.float32
I32 = mybir.dt.int32
U32 = mybir.dt.uint32
F16 = mybir.dt.float16
ALU = mybir.AluOpType
ACT = mybir.ActivationFunctionType
AX_X = mybir.AxisListType.X

P = 128
EPS = 1e-5

NODE_BLOCK = 125
WINDOWS = 11
WIN_TILES = 2
ACT_SHARE = (4, 11)

STEPS = 25
WARM_FROM = 4
UNROLL = 4
STATE_TOL = 2.0 ** -18


def bass_gnn_lstm_kernel(nc, x, src, dst, w_gnn, b_gnn, U_i, V_i, b_i, U_c, V_c, b_c, U_o, V_o, b_o, out):
    N, D = x.shape
    E = src.shape[0]
    H = U_i.shape[1]
    DH = D // P
    HH = H // P
    CHUNKS = N // STEPS
    NB = NODE_BLOCK
    BLOCKS = N // NB
    CPB = NB // STEPS
    EDGE_ROWS = 125
    EDGE_COLS = E // EDGE_ROWS
    WIN_EDGES = WIN_TILES * P
    NW = BLOCKS * WINDOWS
    WIN_BATCHES = -(-NW // P)
    WIN_ROWS = -(-NW // WIN_BATCHES)
    NWP = WIN_BATCHES * WIN_ROWS
    SPAN = [NB * (w + 1) // WINDOWS - NB * w // WINDOWS for w in range(NW)]
    WIN_MAX = max(SPAN)
    LINE = 2 * D + 2
    MT = 3 * HH
    G_RUN = 8
    X_CHUNK = 5
    COLS = [(0, (CHUNKS + 1) // 2), ((CHUNKS + 1) // 2, CHUNKS)]
    assert N == CHUNKS * STEPS == BLOCKS * NB and NB == CPB * STEPS and CHUNKS <= P
    assert D == DH * P and H == HH * P and D == H
    assert EDGE_COLS % 2 == 1
    assert E == EDGE_ROWS * EDGE_COLS and BLOCKS % X_CHUNK == 0 and WIN_MAX * BLOCKS <= 512 and NWP <= 512

    h_dram = nc.dram_tensor("h_dram", (N, LINE), F16, kind="Internal").ap()

    with ExitStack() as ctx:
        def sb(name, shape, dt=F32):
            return ctx.enter_context(nc.sbuf_tensor(name, shape, dt))

        def ps(name, shape, dt=F32):
            return ctx.enter_context(nc.psum_tensor(name, shape, dt))

        def sem(name):
            return ctx.enter_context(nc.semaphore(name))

        x_sb = sb("x_sb", [NB, BLOCKS, D])
        gx = sb("gx", [P, STEPS, MT, CHUNKS])
        gx_flat = gx[:, :, :, :].rearrange("p s m k -> p (s m k)")
        at = [0]

        def early(parts, n, dt=F32):
            a = gx_flat[0:parts, at[0]:at[0] + n]
            at[0] += n
            return a if dt == F32 else a.bitcast(dt)
        dst_rows = early(EDGE_ROWS, EDGE_COLS, I32)
        first_row = early(EDGE_ROWS, 1)
        before = early(EDGE_ROWS, NWP)
        row_f = early(WIN_ROWS, WIN_BATCHES)
        row_i = early(WIN_ROWS, WIN_BATCHES, I32)
        win_rows = early(WIN_ROWS, WIN_BATCHES * EDGE_COLS, I32).rearrange("p (b e) -> p b e", b=WIN_BATCHES)
        win_rows_f = early(WIN_ROWS, WIN_BATCHES * EDGE_COLS).rearrange("p (b e) -> p b e", b=WIN_BATCHES)
        in_row = early(WIN_ROWS, WIN_BATCHES)
        start_f = early(WIN_ROWS, WIN_BATCHES)
        start_i = early(WIN_ROWS, WIN_BATCHES, I32)
        win_edges = early(WIN_ROWS, 2 * WIN_BATCHES * WIN_EDGES, I32).rearrange(
            "p (a b e) -> p a b e", a=2, b=WIN_BATCHES)
        win_edges_f = early(WIN_ROWS, 2 * WIN_BATCHES * WIN_EDGES).rearrange(
            "p (a b e) -> p a b e", a=2, b=WIN_BATCHES)
        col_thr = early(WIN_ROWS, WIN_BATCHES)
        row_thr = early(P, NWP + 1)
        limit = early(P, NWP)
        rel = early(P, WIN_TILES * NWP).rearrange("p (t w) -> p t w", t=WIN_TILES)
        slot = early(P, WIN_TILES * NWP).rearrange("p (t w) -> p t w", t=WIN_TILES)
        inside = early(P, WIN_TILES * NWP).rearrange("p (t w) -> p t w", t=WIN_TILES)
        z = early(NB, 4 * D).rearrange("p (b d) -> p b d", b=4)
        zT = early(P, 3 * DH * NB, F16).rearrange("p (b c d n) -> p b c d n", b=3, c=2, d=DH)
        w_sb = early(P, DH * D).rearrange("p (d h) -> p d h", d=DH)
        h_all = sb("h_all", [P, STEPS + 1, HH, CHUNKS])
        c_all = sb("c_all", [P, STEPS + 1, HH, CHUNKS])
        h_flat = h_all[:, :, :, :].rearrange("p s m k -> p (s m k)")
        c_flat = c_all[:, :, :, :].rearrange("p s m k -> p (s m k)")
        gap = sb("gap", [P, 2, HH, CHUNKS - 1])
        line = c_flat[0:NB, 0:BLOCKS * LINE // 2].bitcast(F16).rearrange("p (j f) -> p j f", f=LINE)
        U_sb = h_flat[:, 0:DH * 3 * H].rearrange("p (d n h) -> p d n h", d=DH, n=3)
        V_sb = h_flat[:, DH * 3 * H:(DH + HH) * 3 * H].rearrange("p (d n h) -> p d n h", d=HH, n=3)
        at[0] = 0

        def general(n, dt=F32):
            at[0] += n
            a = h_flat[0:EDGE_ROWS, at[0] - n:at[0]]
            return a if dt == F32 else a.bitcast(dt)
        g_dst = general(EDGE_COLS, I32)
        g_src = general(EDGE_COLS, I32)
        g_dst_f = general(EDGE_COLS)
        g_rel = general(EDGE_COLS)
        g_src_now = general(2, I32)
        g_hot = general(P, F16).rearrange("p (b n) -> p b n", b=2)
        g_rows = general(LINE, F16).rearrange("p (b f) -> p b f", b=2)
        counts_all = sb("counts", [P, 2, BLOCKS, P], F16)
        counts = counts_all[0:NB, :, :, :]
        HOTS = 6
        hot_p = sb("hot_p", [P, HOTS, WIN_TILES, P], F16)
        hot_ts = sb("hot_ts", [P, HOTS, WIN_TILES, WIN_MAX * BLOCKS + 4], F16)
        key = sb("key", [P, WIN_TILES, NWP])
        part = sb("part", [P, WIN_TILES, NWP])
        iota = sb("iota", [P, 512], F16)
        covered = sb("covered", [P, 1])
        open_f = sb("open_f", [1, 1])
        open_i = sb("open_i", [1, 1], I32)
        ones = sb("ones", [P, 1])
        ident = sb("ident", [P, P])
        b_bc = sb("b_bc", [NB, D])
        has = sb("has", [NB, 1])
        inv = sb("inv", [NB, 1])
        W16 = sb("W16", [P, 2, DH, D], F16)
        U16 = sb("U16", [P, 2, DH, 3 * H], F16)
        V16 = sb("V16", [P, 2, HH, 3 * H], F16)
        w_max = sb("w_max", [P, 3])
        w_min = sb("w_min", [P, 3])
        w_top = sb("w_top", [P, 3])
        w_exp = sb("w_exp", [P, 3], I32)
        w_scale = sb("w_scale", [P, 3])
        w_unscale = sb("w_unscale", [P, 3])
        h16 = sb("h16", [P, 2, HH, CHUNKS], F16)
        gb = sb("gb", [P, 3, HH])
        gx_scale = sb("gx_scale", [P, 1])
        stats = sb("stats", [NB, BLOCKS, 6])
        mv = sb("mv", [NB, BLOCKS, 2])
        rstd = sb("rstd", [NB, BLOCKS])
        var_eps = sb("var_eps", [NB, BLOCKS])
        sd = sb("sd", [NB, BLOCKS])
        newton = sb("newton", [NB, BLOCKS])
        shift = sb("shift", [NB, BLOCKS])
        z2 = sb("z2", [NB, 2, D])
        TB = 4
        z2T = sb("z2T", [P, 2, 2, DH, TB, NB], F16)
        at[0] = 0
        half = counts_all[:, :, :, :].rearrange("p b s n -> p (b s n)").bitcast(F32)

        def of_step(m):
            n = 2 * m * COLS[0][1]
            at[0] += n
            return half[:, at[0] - n:at[0]].rearrange("p (q m k) -> p q m k", q=2, m=m)
        gate, ig, hc, tc = of_step(MT), of_step(HH), of_step(HH), of_step(HH)
        h_out = half[:, at[0]:at[0] + 3 * HH * NB].rearrange("p (b m n) -> p b m n", b=3, m=HH)
        near = sb("near", [P, 1])
        far_f = sb("far_f", [1, 1])
        far_i = sb("far_i", [1, 1], I32)

        bank = [ps(f"bank{i}", [P, 512]) for i in range(8)]
        ps_count = [bank[2], bank[3], bank[4]]
        ps_sum = [bank[0], bank[1]]
        ps_zT = bank[5]
        ps_gates = [bank[6], bank[7]]
        ps_g = [bank[0], bank[1]]
        ps_x = [bank[6], bank[7]]
        ps_t = [bank[2], bank[3]]
        ps_out = bank[2:6]

        x_in = [sem(f"x_in{c}") for c in range(BLOCKS // X_CHUNK)]
        dst_rows_in = sem("dst_rows_in")
        w_in = sem("w_in")
        weights_in = sem("weights_in")
        b_in = sem("b_in")
        ident_zero = sem("ident_zero")
        iotas = sem("iotas")
        consts = sem("consts")
        dve_seq = sem("dve_seq")
        before_ready = sem("before_ready")
        before_ps = sem("before_ps")
        rows_known = sem("rows_known")
        win_rows_in = [sem(f"win_rows_in{b}") for b in range(WIN_BATCHES)]
        starts_known = sem("starts_known")
        win_edges_in = [[sem(f"win_edges_in{a}_{b}") for b in range(WIN_BATCHES)] for a in range(2)]
        edges_f = sem("edges_f")
        edges_ps = sem("edges_ps")
        keys_ready = sem("keys_ready")
        covered_ready = sem("covered_ready")
        covered_ps = sem("covered_ps")
        open_ready = sem("open_ready")
        w_max_ready = sem("w_max_ready")
        w_max_all = sem("w_max_all")
        scales_ready = sem("scales_ready")
        unscales_ready = sem("unscales_ready")
        gx_scales_ready = sem("gx_scales_ready")
        w_hi = sem("w_hi")
        w_split = sem("w_split")
        uv_hi = sem("uv_hi")
        uv_split = sem("uv_split")
        rstd_ready = sem("rstd_ready")
        var_ready = sem("var_ready")
        sqrt_ready = sem("sqrt_ready")
        stats_ready = sem("stats_ready")
        newton_seq = sem("newton_seq")
        aggregated = sem("aggregated")
        z_ready = sem("z_ready")
        zT_ps = sem("zT_ps")
        zT_hi = sem("zT_hi")
        zT_ready = sem("zT_ready")
        line_ps = sem("line_ps")
        line_hi = sem("line_hi")
        line_ready = sem("line_ready")
        hot_p_act = sem("hot_p_act")
        hot_ready = sem("hot_ready")
        hot_squared = sem("hot_squared")
        count_ps = sem("count_ps")
        counted = sem("counted")
        sum_ps = sem("sum_ps")
        x1_ready = sem("x1_ready")
        z2_ready = sem("z2_ready")
        z2T_ps = sem("z2T_ps")
        z2T_hi = sem("z2T_hi")
        z2T_ready = sem("z2T_ready")
        gx_ps = sem("gx_ps")
        gx_ready = sem("gx_ready")
        h_out_ready = sem("h_out_ready")
        g_in = sem("g_in")
        g_line_out = sem("g_line_out")
        g_seq = sem("g_seq")
        g_src_copied = sem("g_src_copied")
        g_rows_in = [[sem(f"g_rows_in{r}_{b}") for b in range(2)] for r in range(-(-BLOCKS // G_RUN))]
        g_hot_ready = sem("g_hot_ready")
        g_used = sem("g_used")
        start_set = sem("start_set")
        start_ready = sem("start_ready")
        ig_ps = [sem(f"ig_ps{i}") for i in range(2)]
        o_ps = [sem(f"o_ps{i}") for i in range(2)]
        bits_set = sem("bits_set")
        ig_seed = [sem(f"ig_seed{i}") for i in range(2)]
        o_seed = [sem(f"o_seed{i}") for i in range(2)]
        ig_gate = [sem(f"ig_gate{i}") for i in range(2)]
        o_gate = [sem(f"o_gate{i}") for i in range(2)]
        hc_ready = [sem(f"hc_ready{i}") for i in range(2)]
        ig_ready = [sem(f"ig_ready{i}") for i in range(2)]
        c_ready = [sem(f"c_ready{i}") for i in range(2)]
        tc_ready = [sem(f"tc_ready{i}") for i in range(2)]
        h_ready = [sem(f"h_ready{i}") for i in range(2)]
        hi_ready = [sem(f"hi_ready{i}") for i in range(2)]
        lo_ready = [sem(f"lo_ready{i}") for i in range(2)]
        waits_passed = sem("waits_passed")
        near_ready = sem("near_ready")
        near_ps = sem("near_ps")
        far_ready = sem("far_ready")
        hT_ready = sem("hT_ready")
        out_ready = sem("out_ready")
        out_done = sem("out_done")

        WARM = STEPS - WARM_FROM
        ROUNDS = [(WARM_FROM, 0), (0, WARM), (0, WARM + STEPS)]
        DONE = WARM + 2 * STEPS
        PRODUCTS = [(0, 0), (1, 0), (0, 1)]
        LAG = 4
        FINISH_AT, ROOT_AT, NORM_AT, TURN_AT, HIGH_AT, LOW_AT = (7, 2), (8, 2), (3, 3), (4, 3), (5, 3), (0, 4)
        ROUND = 3.0 * 2.0 ** 22
        BATCHES = [(b, min(b + TB, BLOCKS)) for b in range(0, BLOCKS, TB)]

        def on_act(w):
            return (w * ACT_SHARE[0]) % ACT_SHARE[1] < ACT_SHARE[0]

        def gates_at(j, i):
            return [(b, (j0, j1), m) for b, (j0, j1) in enumerate(BATCHES) for m in range(MT)
                    if (j, i) == ((j1 + 3 + m // 2, (1, 6)[m % 2]) if j1 + 3 < BLOCKS else (j1 + 3, (1, 1, 2, 5, 5, 6)[m]))]

        def where_open(eng, run_block, start=None):
            eng.wait_ge(open_ready, 1)
            with eng.If(eng.value_load(open_i[0:1, 0:1], min_val=0, max_val=1) > 0):
                if start:
                    start()
                for j in range(BLOCKS):
                    run_block(j)

        def tiles_of(eng, one):
            one(0, 0)
            with eng.Fori(0, (EDGE_COLS - 3) // 2) as i:
                one(i * 2 + 1, 1)
                one(i * 2 + 2, 0)
            one(EDGE_COLS - 2, 1)
            one(EDGE_COLS - 1, 0)

        block = ctx.enter_context(nc.Block())

        @block.sync
        def _(sp):
            sp.dma_start(dst_rows, dst.rearrange("(r c) -> r c", c=EDGE_COLS)).then_inc(dst_rows_in, 16)
            x_rows = x.rearrange("(j p) d -> p j d", p=NB)
            for c in range(BLOCKS // X_CHUNK):
                js = slice(c * X_CHUNK, (c + 1) * X_CHUNK)
                sp.dma_start(x_sb[:, js, :], x_rows[:, js, :]).then_inc(x_in[c], 16)
            with nc.allow_non_contiguous_dma("bias to every partition"):
                sp.dma_start(b_bc[:, :], b_gnn.partition_broadcast(NB)).then_inc(b_in, 16)
            sp.wait_ge(open_ready, 1)
            with sp.If(sp.value_load(open_i[0:1, 0:1], min_val=0, max_val=1) > 0):
                sp.wait_ge(gx_ready, MT * len(BATCHES))
                sp.dma_start(h_dram.rearrange("(j p) f -> p j f", p=NB), line).then_inc(g_line_out, 16)
                sp.dma_start(x_sb[:, :, :], x_rows).then_inc(g_in, 16)
                sp.dma_start(g_dst, dst.rearrange("(r c) -> r c", c=EDGE_COLS)).then_inc(g_in, 16)
                sp.dma_start(g_src, src.rearrange("(r c) -> r c", c=EDGE_COLS)).then_inc(g_in, 16)
            out_rows = out.rearrange("(j p) d -> p j d", p=NB)
            ends = list(range(X_CHUNK, BLOCKS, X_CHUNK)) + [BLOCKS - 3, BLOCKS - 1, BLOCKS]
            for j0, j1 in zip([0] + ends, ends):
                sp.wait_ge(out_ready, j1)
                sp.dma_start(out_rows[:, j0:j1, :], x_sb[:, j0:j1, :]).then_inc(out_done, 16)
            sp.wait_ge(out_done, 16 * len(ends))

        def steps_of(eng, first, done):
            if isinstance(done, int):
                yield from range(first + 1, STEPS - UNROLL + 1, UNROLL)
            else:
                with eng.Fori(first + 1, STEPS - UNROLL + 1, UNROLL) as s:
                    yield s

        def at_each_round(eng, run_round, count_near=None):
            for n, (first, done) in enumerate(ROUNDS):
                run_round(first, done, n + 1)
            if count_near:
                count_near()
            eng.wait_ge(far_ready, 1)
            far = eng.value_load(far_i[0:1, 0:1], min_val=0, max_val=1)
            with eng.If(far > 0):
                with eng.Fori(0, CHUNKS) as r:
                    run_round(0, r * STEPS + DONE, r + (len(ROUNDS) + 1))

        @block.gpsimd
        def _(pool):
            nc.gpsimd.iota(row_thr, pattern=[[1, NWP + 1]], base=0, channel_multiplier=0,
                           allow_small_or_imprecise_dtypes=True).then_inc(iotas, 1)
            nc.gpsimd.iota(col_thr, pattern=[[WIN_ROWS, WIN_BATCHES]], base=0, channel_multiplier=1,
                           allow_small_or_imprecise_dtypes=True).then_inc(iotas, 1)
            nc.gpsimd.memset(ones[:, :], 1.0).then_inc(consts, 1)
            nc.gpsimd.memset(ident[:, :], 0.0).then_inc(ident_zero, 1)
            pool.wait_ge(ident_zero, 1)
            nc.gpsimd.affine_select(out=ident[:, :], in_=ident[:, :], compare_op=ALU.not_equal, fill=1.0, base=0,
                                    pattern=[[-1, P]], channel_multiplier=1).then_inc(consts, 1)
            nc.gpsimd.iota(iota[:, :], pattern=[[1, 512]], base=0, channel_multiplier=0,
                           allow_small_or_imprecise_dtypes=True).then_inc(consts, 1)
            nc.gpsimd.memset(counts, 0.0).then_inc(consts, 1)
            nc.gpsimd.memset(line[:, :, 2 * D:LINE], 1.0).then_inc(consts, 1)
            pool.wait_ge(rows_known, 1)
            for b in range(WIN_BATCHES):
                pool.indirect_dma_start(
                    win_rows[:, b, :], None, dst.rearrange("(r c) -> r c", c=EDGE_COLS),
                    bass.IndirectOffsetOnAxis(ap=row_i[:, b:b + 1].bitcast(U32), axis=0),
                ).then_inc(win_rows_in[b], 16)

            def weights_top(n, n0, n1):
                pool.wait_ge(w_max_ready, n)
                nc.gpsimd.partition_all_reduce(w_top[:, n0:n1], w_max[:, n0:n1], P, bass.bass_isa.ReduceOp.max
                                               ).then_inc(w_max_all, 1)

            weights_top(1, 0, 1)
            pool.wait_ge(starts_known, 1)
            for a, t in enumerate((dst, src)):
                for b in range(WIN_BATCHES):
                    pool.indirect_dma_start(
                        win_edges[:, a, b, :], None,
                        t.rearrange("(e a) -> e a", a=1),
                        bass.IndirectOffsetOnAxis(ap=start_i[:, b:b + 1].bitcast(U32), axis=0),
                    ).then_inc(win_edges_in[a][b], 16)
            weights_top(2, 1, 3)

            def general_block(j):
                if j == 0:
                    pool.wait_ge(g_line_out, 16)
                    pool.wait_ge(g_in, 48)

                def one(e, b):
                    turn = e + j * EDGE_COLS
                    if not isinstance(e, int) or turn >= 2:
                        pool.wait_ge(g_used, turn - (0 if isinstance(e, int) and e == 0 else 1))
                        pool.sem_inc(waits_passed)
                    nc.gpsimd.tensor_copy(g_src_now[:, b:b + 1], g_src[:, bass.ds(e, 1)]).then_inc(g_src_copied, 1)
                    pool.wait_ge(g_src_copied, turn + 1)
                    pool.sem_inc(waits_passed)
                    pool.indirect_dma_start(
                        g_rows[:, b, :], None, h_dram,
                        bass.IndirectOffsetOnAxis(ap=g_src_now[:, b:b + 1].bitcast(U32), axis=0),
                    ).then_inc(g_rows_in[j // G_RUN][b], 16)
                tiles_of(pool, one)

            where_open(pool, general_block)

            def low_part(q, slot, seen):
                c0, c1 = COLS[q]
                pool.wait_ge(h_ready[q], seen)
                pool.wait_ge(hi_ready[q], seen)
                nc.gpsimd.tensor_tensor(h16[:, 1, :, c0:c1], h_all[:, slot, :, c0:c1], h16[:, 0, :, c0:c1],
                                        ALU.subtract).then_inc(lo_ready[q], 1)

            def old_part(q, slot):
                c0, c1 = COLS[q]
                nc.gpsimd.tensor_tensor(hc[:, q, :, 0:c1 - c0], h_all[:, slot, :, c0:c1], c_all[:, slot, :, c0:c1],
                                        ALU.mult).then_inc(hc_ready[q], 1)

            def rough_round(first):
                pool.wait_ge(start_ready, 1)
                for s in range(first, STEPS):
                    for q, (c0, c1) in enumerate(COLS):
                        pool.wait_ge(hi_ready[q], s - first + 1)
                        nc.gpsimd.tensor_tensor(hc[:, q, :, 0:c1 - c0], h16[:, 0, :, c0:c1], c_all[:, s, :, c0:c1],
                                                ALU.mult).then_inc(hc_ready[q], 1)
                for q in range(2):
                    pool.sem_inc(lo_ready[q], STEPS - first + (1 - q))

            def run_round(first, done, starts):
                if first > 0:
                    return rough_round(first)
                pool.wait_ge(start_ready, starts)
                pool.sem_inc(waits_passed)

                def step(s, seen):
                    old_part(0, bass.ds(s, 1))
                    low_part(1, bass.ds(s, 1), seen)
                    old_part(1, bass.ds(s, 1))
                    low_part(0, bass.ds(s + 1, 1), seen + 1)

                low_part(0, slice(first, first + 1), done + starts)
                step(first, done + starts)
                for s in steps_of(pool, first, done):
                    for u in range(UNROLL):
                        step(s + u, s + (done - first + starts + u))

            at_each_round(pool, run_round)

        @block.scalar
        def _(act):
            act.dma_start(w_sb, w_gnn.rearrange("(a p) h -> p a h", p=P)).then_inc(w_in, 16)
            for n, (U, V, b) in enumerate(((U_i, V_i, b_i), (U_c, V_c, b_c), (U_o, V_o, b_o))):
                act.dma_start(U_sb[:, :, n, :], U.rearrange("(a p) h -> p a h", p=P)).then_inc(weights_in, 16)
                act.dma_start(V_sb[:, :, n, :], V.rearrange("(a p) h -> p a h", p=P)).then_inc(weights_in, 16)
                with nc.allow_non_contiguous_dma("bias columns"):
                    act.dma_start(gb[:, n, :], b.rearrange("(a p) -> p a", p=P)).then_inc(weights_in, 16)

            sqrts = [0]

            def deviation(j0, j1):
                sqrts[0] += 1
                act.wait_ge(var_ready, sqrts[0])
                nc.scalar.activation(sd[:, j0:j1], var_eps[:, j0:j1], ACT.Sqrt).then_inc(sqrt_ready, 1)

            def first_norm(j):
                act.wait_ge(rstd_ready, j // X_CHUNK + 1)
                if j >= 4:
                    act.wait_ge(zT_ps, j - 3)
                nc.scalar.activation(z[:, j % 4, :], x_sb[:, j, :], ACT.Identity, bias=shift[:, j:j + 1],
                                     scale=rstd[:, j:j + 1]).then_inc(z_ready, 1)

            for c in range(2):
                deviation(c * X_CHUNK, (c + 1) * X_CHUNK)
            for c in range(BLOCKS // X_CHUNK):
                if c > 0 and (c + 2) * X_CHUNK <= BLOCKS:
                    deviation((c + 1) * X_CHUNK, (c + 2) * X_CHUNK)
                for j in range(c * X_CHUNK, (c + 1) * X_CHUNK + (2 if (c + 1) * X_CHUNK == BLOCKS else 0)):
                    if j == 0:
                        act.wait_ge(scales_ready, 1)
                        nc.scalar.activation(W16[:, 0, :, :], w_sb, ACT.Copy, scale=w_scale[:, 0:1]
                                             ).then_inc(w_hi, 1)
                    if j == 0:
                        first_norm(0)
                    if j + 1 < BLOCKS:
                        first_norm(j + 1)
                    if j < BLOCKS:
                        act.wait_ge(zT_ps, j + 1)
                        if j >= 3:
                            act.wait_ge(line_ps, j - 2)
                        nc.scalar.activation(zT[:, j % 3, 0, :, :],
                                             bank[5 + j % 2][:, 0:DH * NB].rearrange("p (d n) -> p d n", d=DH),
                                             ACT.Copy).then_inc(zT_hi, 1)
                    if j >= 2:
                        act.wait_ge(line_ps, j - 1)
                        nc.scalar.activation(line[:, j - 2, D:2 * D], bank[(j - 2) % 2][0:NB, 0:D], ACT.Copy
                                             ).then_inc(line_hi, 1)

            tile = 0

            def gates_out(j0, j1, tiles=range(MT)):
                nonlocal tile
                if tile == 0:
                    act.wait_ge(gx_scales_ready, 2)
                for m in tiles:
                    act.wait_ge(gx_ps, tile + 1)
                    nc.scalar.activation(gx[:, :, m, j0 * CPB:j1 * CPB],
                                         ps_gates[tile % 2][:, 0:(j1 - j0) * NB].rearrange("p (k s) -> p s k",
                                                                                           s=STEPS),
                                         ACT.Identity, bias=gb[:, m // HH, m % HH:m % HH + 1],
                                         scale=gx_scale[:, 0:1]).then_inc(gx_ready, 1)
                    tile += 1

            squared = [0]

            def source_one_hots(w):
                if w >= NW or not on_act(w):
                    return
                for t in range(WIN_TILES):
                    nc.scalar.activation(hot_p[:, w % HOTS, t, :], iota[:, 0:P], ACT.Square, scale=-1.0,
                                         bias=part[:, t, w:w + 1]).then_inc(hot_squared, 1)
                squared[0] += WIN_TILES
                act.wait_ge(hot_squared, squared[0])
                nc.scalar.activation(hot_p[:, w % HOTS, :, :], hot_p[:, w % HOTS, :, :], ACT.Relu, scale=-1.0,
                                     bias=ones[:, 0:1]).then_inc(hot_p_act, 1)

            act.wait_ge(consts, 5)
            act.wait_ge(keys_ready, 1)
            for w in range(HOTS - 1):
                source_one_hots(w)

            for j in range(BLOCKS + LAG):
                if j == 3:
                    act.wait_ge(scales_ready, 2)
                    for n in range(3):
                        for u, (w, w16) in enumerate(((U_sb, U16), (V_sb, V16))):
                            nc.scalar.activation(w16[:, 0, :, n * H:(n + 1) * H], w[:, :, n, :], ACT.Copy,
                                                 scale=w_scale[:, 1 + u:2 + u]).then_inc(uv_hi, 1)
                for i in range(WINDOWS):
                    w = j * WINDOWS + i
                    if j < BLOCKS:
                        act.wait_ge(count_ps, w + 1)
                        if i == 0 and j >= 2:
                            act.wait_ge(sum_ps, j - 1)
                        n0 = NB * i // WINDOWS
                        n = SPAN[w]
                        nc.scalar.activation(counts[:, j % 2, :, n0:n0 + n],
                                             ps_count[w % 3][0:NB, 0:n * BLOCKS].rearrange("p (n s) -> p s n", n=n),
                                             ACT.Copy).then_inc(counted, 1)
                        source_one_hots(w + HOTS - 1)
                    for _, (j0, j1), m in gates_at(j, i - 1):
                        gates_out(j0, j1, [m])
                    t = j - ROOT_AT[1]
                    if i == ROOT_AT[0] and 0 <= t < BLOCKS:
                        deviation(t, t + 1)
                    t = j - HIGH_AT[1]
                    if i == HIGH_AT[0] and 0 <= t < BLOCKS:
                        act.wait_ge(z2T_ps, t + 1)
                        if t >= 2 * TB and t % TB == 0:
                            act.wait_ge(gx_ps, MT * (t // TB - 1))
                        nc.scalar.activation(z2T[:, (t // TB) % 2, 0, :, t % TB, :],
                                             ps_zT[:, 0:DH * NB].rearrange("p (d n) -> p d n", d=DH),
                                             ACT.Copy).then_inc(z2T_hi, 1)

            def general_block(j):
                deviation(j, j + 1)
                act.wait_ge(z2T_ps, BLOCKS + j + 1)
                nc.scalar.activation(z2T[:, 0, 0, :, 0, :],
                                     ps_zT[:, 0:DH * NB].rearrange("p (d n) -> p d n", d=DH),
                                     ACT.Copy).then_inc(z2T_hi, 1)
                gates_out(j, j + 1)

            where_open(act, general_block)

            def run_round(first, done, starts):
                ahead = isinstance(done, int)

                def seed(q, s, turn):
                    c0, c1 = COLS[q]
                    n = c1 - c0
                    if not isinstance(turn, int) or turn > 1:
                        act.wait_ge(ig_gate[q], turn - 1)
                    if not isinstance(turn, int):
                        act.sem_inc(waits_passed)
                    nc.scalar.activation(ps_g[q][:, 0:2 * HH * n].rearrange("p (m k) -> p m k", k=n),
                                         gx[:, bass.ds(s, 1), 0:2 * HH, c0:c1], ACT.Copy).then_inc(ig_seed[q], 1)
                    if not isinstance(turn, int) or turn > 1:
                        act.wait_ge(o_gate[q], turn - 1)
                    if not isinstance(turn, int):
                        act.sem_inc(waits_passed)
                    nc.scalar.activation(ps_x[q][:, 0:HH * n].rearrange("p (m k) -> p m k", k=n),
                                         gx[:, bass.ds(s, 1), 2 * HH:MT, c0:c1], ACT.Copy).then_inc(o_seed[q], 1)

                def gates(q, s, turn):
                    c0, c1 = COLS[q]
                    n = c1 - c0
                    act.wait_ge(ig_ps[q], turn)
                    nc.scalar.activation(gate[:, q, 0:2 * HH, 0:n],
                                         ps_g[q][:, 0:2 * HH * n].rearrange("p (m k) -> p m k", k=n), ACT.Tanh,
                                         scale=w_unscale[:, 2:3]).then_inc(ig_gate[q], 1)
                    act.wait_ge(o_ps[q], turn)
                    nc.scalar.activation(gate[:, q, 2 * HH:MT, 0:n],
                                         ps_x[q][:, 0:HH * n].rearrange("p (m k) -> p m k", k=n), ACT.Tanh,
                                         scale=w_unscale[:, 2:3]).then_inc(o_gate[q], 1)
                    if ahead and s + 1 < STEPS:
                        seed(q, s + 1, turn + 1)
                    act.wait_ge(c_ready[q], turn)
                    nc.scalar.activation(tc[:, q, :, 0:n], c_all[:, bass.ds(s + 1, 1), :, c0:c1], ACT.Tanh,
                                         scale=0.5).then_inc(tc_ready[q], 1)

                for q in range(2):
                    seed(q, first, done + 1)
                gates(0, first, done + 1)
                for s in steps_of(act, first, done):
                    for u in range(UNROLL):
                        turn = s + (done - first + 1 + u)
                        if not ahead:
                            seed(0, s + u, turn)
                        gates(1, s + (u - 1), s + (done - first + u))
                        if not ahead:
                            seed(1, s + u, turn)
                        gates(0, s + u, turn)
                gates(1, STEPS - 1, done + STEPS - first)

            act.wait_ge(bits_set, 1)
            at_each_round(act, run_round)

            for j in range(BLOCKS):
                if j >= 3:
                    act.wait_ge(hT_ready, j - 2)
                nc.scalar.activation(h_out[:, j % 3, :, :].rearrange("p m (k s) -> p m k s", s=STEPS),
                                     h_all[:, 1:STEPS + 1, :, j * CPB:(j + 1) * CPB].rearrange("p s m k -> p m k s"),
                                     ACT.Copy).then_inc(h_out_ready, 1)

        @block.tensor
        def _(pe):
            pe.wait_ge(consts, 5)
            pe.wait_ge(before_ready, 1)
            for b in range(WIN_BATCHES):
                mm = nc.tensor.matmul(bank[7][0:WIN_ROWS, b:b + 1], before[:, b * WIN_ROWS:(b + 1) * WIN_ROWS],
                                      ones[0:EDGE_ROWS, 0:1], start=True, stop=True)
            mm.then_inc(before_ps, 1)

            for j in range(BLOCKS + 2):
                if j < BLOCKS:
                    pe.wait_ge(z_ready, j + 1)
                    if j >= 2:
                        pe.wait_ge(zT_ready, j - 1)
                    for d in range(DH):
                        mm = nc.tensor.transpose(bank[5 + j % 2][:, d * NB:(d + 1) * NB],
                                                 z[:, j % 4, d * P:(d + 1) * P], ident[0:NB, 0:NB])
                    mm.then_inc(zT_ps, 1)
                if j >= 2:
                    t = j - 2
                    pe.wait_ge(zT_ready, t + 1)
                    if t == 0:
                        pe.wait_ge(w_split, 1)
                    if t >= 2:
                        pe.wait_ge(line_ready, t - 1)
                    parts = [(d, w_part, z_part) for w_part, z_part in PRODUCTS for d in range(DH)]
                    for n, (d, w_part, z_part) in enumerate(parts):
                        mm = nc.tensor.matmul(bank[t % 2][0:NB, 0:D], zT[:, t % 3, z_part, d, :],
                                              W16[:, w_part, d, :], start=(n == 0), stop=(n == len(parts) - 1))
                    mm.then_inc(line_ps, 1)

            pe.wait_ge(edges_f, 1)
            for a in range(2):
                for t in range(WIN_TILES):
                    for b in range(WIN_BATCHES):
                        mm = nc.tensor.transpose(bank[2 + 2 * a + t][:, b * WIN_ROWS:(b + 1) * WIN_ROWS],
                                                 win_edges_f[:, a, b, t * P:(t + 1) * P],
                                                 ident[0:WIN_ROWS, 0:WIN_ROWS])
            mm.then_inc(edges_ps, 1)

            def sums(j, s):
                nc.tensor.matmul(ps_sum[j % 2][:, 0:D + 1], counts[:, j % 2, s, :], line[:, s, D:2 * D + 1],
                                 start=(s == 0), stop=False, skip_group_check=True)
                return nc.tensor.matmul(ps_sum[j % 2][:, 0:D], counts[:, j % 2, s, :], line[:, s, 0:D],
                                        start=False, stop=(s == BLOCKS - 1), skip_group_check=True)

            def turn_z2(t):
                pe.wait_ge(z2_ready, t + 1)
                if t >= 1:
                    pe.wait_ge(z2T_ready, t)
                for d in range(DH):
                    mm = nc.tensor.transpose(ps_zT[:, d * NB:(d + 1) * NB], z2[:, t % 2, d * P:(d + 1) * P],
                                             ident[0:NB, 0:NB])
                mm.then_inc(z2T_ps, 1)

            tile = 0

            def gates_x(n_blocks, buf, turned, tiles=range(MT)):
                nonlocal tile
                pe.wait_ge(z2T_ready, turned)
                if tile == 0:
                    pe.wait_ge(uv_split, 6)
                for m in tiles:
                    if tile >= 2:
                        pe.wait_ge(gx_ready, tile - 1)
                    parts = [(d, w_part, z_part) for w_part, z_part in PRODUCTS for d in range(DH)]
                    for n, (d, w_part, z_part) in enumerate(parts):
                        mm = nc.tensor.matmul(ps_gates[tile % 2][:, 0:n_blocks * NB],
                                              U16[:, w_part, d, m * P:(m + 1) * P],
                                              z2T[:, buf, z_part, d, 0:n_blocks, :].rearrange("p s k -> p (s k)"),
                                              start=(n == 0), stop=(n == len(parts) - 1))
                    mm.then_inc(gx_ps, 1)
                    tile += 1

            pe.wait_ge(keys_ready, 1)
            pe.wait_ge(line_ready, BLOCKS)
            pooled = 0
            for j in range(BLOCKS + LAG):
                for i in range(WINDOWS):
                    w = j * WINDOWS + i
                    if j < BLOCKS:
                        pe.wait_ge(hot_ready, w + 1)
                        if on_act(w):
                            pooled += 1
                            pe.wait_ge(hot_p_act, pooled)
                        if w >= 3:
                            pe.wait_ge(counted, w - 2)
                        n = SPAN[w] * BLOCKS
                        for t in range(WIN_TILES):
                            mm = nc.tensor.matmul(ps_count[w % 3][:, 0:n], hot_p[:, w % HOTS, t, :],
                                                  hot_ts[:, w % HOTS, t, 0:n], start=(t == 0),
                                                  stop=(t == WIN_TILES - 1))
                        mm.then_inc(count_ps, 1)
                    for b, (j0, j1), m in gates_at(j, i):
                        gates_x(j1 - j0, b % 2, j1, [m])
                    if 1 <= j <= BLOCKS:
                        if i == 0:
                            pe.wait_ge(counted, j * WINDOWS)
                            if j >= 3:
                                pe.wait_ge(x1_ready, j - 2)
                        for s in range(BLOCKS * i // WINDOWS, BLOCKS * (i + 1) // WINDOWS):
                            mm = sums(j - 1, s)
                        if i == WINDOWS - 1:
                            mm.then_inc(sum_ps, 1)
                    if i == TURN_AT[0] and 0 <= j - TURN_AT[1] < BLOCKS:
                        turn_z2(j - TURN_AT[1])
            pe.wait_ge(covered_ready, 1)
            nc.tensor.matmul(ps_t[0][0:1, 0:1], covered[:, :], ones[:, 0:1], start=True, stop=True
                             ).then_inc(covered_ps, 1)

            def general_block(j):
                turn_block = BLOCKS + j
                bank_sum = ps_sum[turn_block % 2]
                pe.wait_ge(x1_ready, turn_block - 1)
                run = j // G_RUN * G_RUN

                def one(e, b):
                    turn = e + j * EDGE_COLS
                    pe.wait_ge(g_hot_ready, turn + 1)
                    per_block = EDGE_COLS // 2 + 1 - b
                    if isinstance(e, int):
                        pe.wait_ge(g_rows_in[j // G_RUN][b], 16 * ((j - run) * per_block + e // 2 + 1))
                    else:
                        pe.wait_ge(g_rows_in[j // G_RUN][b], e * 8 + (16 * (j - run) * per_block + 8 * (2 - b)))
                    first, last = (isinstance(e, int) and e == v for v in (0, EDGE_COLS - 1))
                    nc.tensor.matmul(bank_sum[:, 0:D + 1], g_hot[:, b, :], g_rows[:, b, D:2 * D + 1],
                                     start=first, stop=False, skip_group_check=True)
                    nc.tensor.matmul(bank_sum[:, 0:D], g_hot[:, b, :], g_rows[:, b, 0:D],
                                     start=False, stop=last, skip_group_check=True).then_inc(g_used, 1)
                tiles_of(pe, one)
                pe.wait_ge(g_used, (j + 1) * EDGE_COLS)
                nc.tensor.matmul(ps_t[0][0:1, 0:1], covered[:, :], ones[:, 0:1], start=True, stop=True
                                 ).then_inc(sum_ps, 1)
                turn_z2(turn_block)
                gates_x(1, 0, turn_block + 1)
                pe.wait_ge(gx_ready, MT * (len(BATCHES) + j + 1))

            where_open(pe, general_block)

            pe.wait_ge(gx_ready, MT * len(BATCHES))
            for q, (c0, c1) in enumerate(COLS):
                for to, m in ((ps_g[q], 2 * HH), (ps_x[q], HH)):
                    mm = nc.tensor.matmul(to[:, 0:m * (c1 - c0)], V16[:, 0, 0, 0:P], V16[:, 0, 0, 0:m * (c1 - c0)],
                                          start=True, stop=True)
            mm.then_inc(bits_set, 1)

            def run_round(first, done, starts):
                rough = first > 0
                products = PRODUCTS[:1] if rough else PRODUCTS

                def multiply(q, m0, m1, to, part):
                    c0, c1 = COLS[q]
                    n = c1 - c0
                    v_part, h_part = part
                    for m in range(m0, m1):
                        for d in range(HH):
                            mm = nc.tensor.matmul(
                                to[:, (m - m0) * n:(m - m0 + 1) * n], V16[:, v_part, d, m * P:(m + 1) * P],
                                h16[:, h_part, d, c0:c1], start=False,
                                stop=(part == products[-1] and d == HH - 1), skip_group_check=True)
                    return mm

                def step(seen, turn):
                    for q in range(2):
                        pe.wait_ge(ig_seed[q], turn)
                        pe.wait_ge(hi_ready[q], seen)
                        for to, m0, m1, done_sem in ((ps_g[q], 0, 2 * HH, ig_ps[q]), (ps_x[q], 2 * HH, MT, o_ps[q])):
                            if m0 > 0:
                                pe.wait_ge(o_seed[q], turn)
                            for part in products:
                                if part[1] == 0:
                                    mm = multiply(q, m0, m1, to, part)
                            if rough:
                                mm.then_inc(done_sem, 1)
                        if rough:
                            continue
                        pe.wait_ge(lo_ready[q], seen if q == 0 else turn)
                        multiply(q, 0, 2 * HH, ps_g[q], products[-1]).then_inc(ig_ps[q], 1)
                        multiply(q, 2 * HH, MT, ps_x[q], products[-1]).then_inc(o_ps[q], 1)

                step(done + starts, done + 1)
                for s in steps_of(pe, first, done):
                    for u in range(UNROLL):
                        step(s + (done - first + starts + u), s + (done - first + 1 + u))

            def count_near():
                pe.wait_ge(near_ready, 1)
                nc.tensor.matmul(ps_t[0][0:1, 0:1], near[:, :], ones[:, 0:1], start=True, stop=True
                                 ).then_inc(near_ps, 1)

            at_each_round(pe, run_round, count_near)

            for j in range(BLOCKS):
                pe.wait_ge(h_out_ready, j + 1)
                if j >= 4:
                    pe.wait_ge(out_ready, j - 3)
                for d in range(HH):
                    mm = nc.tensor.transpose(ps_out[j % 4][0:NB, d * P:(d + 1) * P], h_out[:, j % 3, d, :],
                                             ident[:, :])
                mm.then_inc(hT_ready, 1)

        @block.vector
        def _(dve):
            seq = [0]

            def flat(w):
                return w[:, :, :, :].rearrange("p d n h -> p (d n h)")

            linked = [dve_seq]

            def link(ins):
                seq[0] += 1
                ins.then_inc(linked[0], 1)
                dve.wait_ge(linked[0], seq[0])

            def norm_stats(s, t):
                link(nc.vector.bn_stats(stats[:, s, :], t))
                nc.vector.bn_aggr(mv[:, s, :], stats[:, s, :]).then_inc(linked[0], 1)
                seq[0] += 1

            sqrts = [0]

            def to_root(j0, j1):
                nc.vector.tensor_scalar(var_eps[:, j0:j1], mv[:, j0:j1, 1], EPS, None, ALU.add
                                        ).then_inc(var_ready, 1)

            def inverse_deviation(j0, j1):
                ve, y, t = var_eps[:, j0:j1], rstd[:, j0:j1], newton[:, j0:j1]
                sqrts[0] += 1
                dve.wait_ge(sqrt_ready, sqrts[0])
                link(nc.vector.reciprocal(y, sd[:, j0:j1]))
                link(nc.vector.tensor_tensor(t, y, y, ALU.mult))
                link(nc.vector.tensor_tensor(t, t, ve, ALU.mult))
                link(nc.vector.tensor_scalar(t, t, -0.5, 1.5, ALU.mult, ALU.add))
                link(nc.vector.tensor_tensor(y, y, t, ALU.mult))

            def whole_part(t, scale, shift):
                link(nc.vector.tensor_scalar(t, t, scale, shift, ALU.mult, ALU.add))
                link(nc.vector.tensor_scalar(t, t, ROUND, None, ALU.add))
                link(nc.vector.tensor_scalar(t, t, ROUND, None, ALU.subtract))

            dve.wait_ge(iotas, 2)
            for t in (row_thr, col_thr):
                whole_part(t, NB / WINDOWS, -(WINDOWS - 1) / (2.0 * WINDOWS))
            dve.wait_ge(dst_rows_in, 16)
            link(nc.vector.tensor_copy(first_row, dst_rows[:, 0:1]))
            nc.vector.tensor_scalar(before, row_thr[0:EDGE_ROWS, 0:NWP], first_row, None, ALU.is_gt
                                    ).then_inc(before_ready, 1)
            link(nc.vector.tensor_tensor(limit, row_thr[:, 1:NWP + 1], row_thr[:, 0:NWP], ALU.subtract))
            link(nc.vector.tensor_scalar(limit, limit, float(BLOCKS), None, ALU.mult))
            dve.wait_ge(before_ps, 1)
            link(nc.vector.tensor_scalar(row_f, bank[7][0:WIN_ROWS, 0:WIN_BATCHES], 1.0, 0.0, ALU.subtract, ALU.max))
            nc.vector.tensor_copy(row_i, row_f).then_inc(rows_known, 1)

            def chunk_stats(j):
                if j % X_CHUNK == 0:
                    dve.wait_ge(x_in[j // X_CHUNK], 16)
                nc.vector.bn_stats(stats[:, j, :], x_sb[:, j, :]).then_inc(stats_ready, 1)

            def chunk_to_root(c):
                for j in range(c * X_CHUNK, (c + 1) * X_CHUNK):
                    dve.wait_ge(stats_ready, j + 1)
                    nc.vector.bn_aggr(mv[:, j, :], stats[:, j, :]).then_inc(aggregated, 1)
                dve.wait_ge(aggregated, (c + 1) * X_CHUNK)
                to_root(c * X_CHUNK, (c + 1) * X_CHUNK)

            def chunk_deviation(c, k):
                js = slice(c * X_CHUNK, (c + 1) * X_CHUNK)
                ve, y, r = var_eps[:, js], rstd[:, js], newton[:, js]
                if k == 0:
                    sqrts[0] += 1
                    dve.wait_ge(sqrt_ready, sqrts[0])
                else:
                    dve.wait_ge(newton_seq, 5 * c + k)
                ins = [lambda: nc.vector.reciprocal(y, sd[:, js]),
                       lambda: nc.vector.tensor_tensor(r, y, y, ALU.mult),
                       lambda: nc.vector.tensor_tensor(r, r, ve, ALU.mult),
                       lambda: nc.vector.tensor_scalar(r, r, -0.5, 1.5, ALU.mult, ALU.add),
                       lambda: nc.vector.tensor_tensor(y, y, r, ALU.mult),
                       lambda: nc.vector.scalar_tensor_tensor(out=shift[:, js], in0=mv[:, js, 0], scalar=-1.0, in1=y,
                                                              op0=ALU.mult, op1=ALU.mult)][k]()
                ins.then_inc(newton_seq if k < 5 else rstd_ready, 1)

            def extreme(to, n, w, op):
                nc.vector.tensor_reduce(to[:, n:n + 1], w, AX_X, op).then_inc(dve_seq, 1)
                seq[0] += 1

            def largest(n0, n1):
                dve.wait_ge(dve_seq, seq[0])
                link(nc.vector.scalar_tensor_tensor(out=w_max[:, n0:n1], in0=w_min[:, n0:n1], scalar=-1.0,
                                                    in1=w_max[:, n0:n1], op0=ALU.mult, op1=ALU.max))
                nc.vector.tensor_scalar(w_max[:, n0:n1], w_max[:, n0:n1], 2.0 ** -100, None, ALU.max
                                        ).then_inc(w_max_ready, 1)

            def scales(n0, n1, top, times):
                dve.wait_ge(w_max_all, times)
                link(nc.vector.tensor_scalar(w_exp[:, n0:n1], w_top[:, n0:n1].bitcast(I32), 0x7F800000, None,
                                             ALU.bitwise_and))
                nc.vector.tensor_scalar(w_unscale[:, n0:n1].bitcast(I32), w_exp[:, n0:n1], -float(top << 23), None,
                                        ALU.add).then_inc(unscales_ready, 1)
                nc.vector.tensor_scalar(w_scale[:, n0:n1].bitcast(I32), w_exp[:, n0:n1], -1.0,
                                        float((127 + 127 + top) << 23), ALU.mult, ALU.add).then_inc(scales_ready, 1)

            def x_scales():
                dve.wait_ge(scales_ready, 2)
                dve.wait_ge(unscales_ready, 2)
                nc.vector.tensor_tensor(gx_scale[:, :], w_unscale[:, 1:2], w_scale[:, 2:3], ALU.mult
                                        ).then_inc(gx_scales_ready, 1)
                nc.vector.tensor_scalar(gb[:, :, :], gb[:, :, :], w_scale[:, 2:3], None, ALU.mult
                                        ).then_inc(gx_scales_ready, 1)

            def halve():
                dve.wait_ge(weights_in, 16 * 9)
                for n, half in ((0, 0.5), (2, 0.5)):
                    nc.vector.tensor_scalar(U_sb[:, :, n, :], U_sb[:, :, n, :], half, None, ALU.mult
                                            ).then_inc(dve_seq, 1)
                    nc.vector.tensor_scalar(gb[:, n, :], gb[:, n, :], half, None, ALU.mult).then_inc(dve_seq, 1)
                    nc.vector.tensor_scalar(V_sb[:, :, n, :], V_sb[:, :, n, :], half * 0.5, None, ALU.mult
                                            ).then_inc(dve_seq, 1)
                    seq[0] += 3
                link(nc.vector.tensor_scalar(V_sb[:, :, 1, :], V_sb[:, :, 1, :], 0.5, None, ALU.mult))

            for c in range(2):
                for j in range(c * X_CHUNK, (c + 1) * X_CHUNK):
                    chunk_stats(j)
                chunk_to_root(c)
            dve.wait_ge(w_in, 16)
            for to, op in ((w_max, ALU.max), (w_min, ALU.min)):
                extreme(to, 0, w_sb.rearrange("p d h -> p (d h)"), op)
            largest(0, 1)

            def window_starts():
                for b in range(WIN_BATCHES):
                    dve.wait_ge(win_rows_in[b], 16)
                for b in range(WIN_BATCHES):
                    nc.vector.tensor_scalar(win_rows_f[:, b, :], win_rows[:, b, :], col_thr[:, b:b + 1], None,
                                            ALU.is_lt).then_inc(dve_seq, 1)
                    seq[0] += 1
                dve.wait_ge(dve_seq, seq[0])
                link(nc.vector.tensor_reduce(in_row, win_rows_f, AX_X, ALU.add))
                link(nc.vector.scalar_tensor_tensor(out=start_f, in0=row_f, scalar=float(EDGE_COLS), in1=in_row,
                                                    op0=ALU.mult, op1=ALU.add))
                link(nc.vector.tensor_scalar(start_f, start_f, float(E - WIN_EDGES), None, ALU.min))
                nc.vector.tensor_copy(start_i, start_f).then_inc(starts_known, 1)

            def window_edges():
                for sems in win_edges_in:
                    for s in sems:
                        dve.wait_ge(s, 16)
                nc.vector.tensor_copy(win_edges_f, win_edges).then_inc(edges_f, 1)

            scales(0, 1, 6, 1)
            for k in range(6):
                chunk_deviation(0, k)
            for c in range(BLOCKS // X_CHUNK):
                for j in range(c * X_CHUNK, (c + 1) * X_CHUNK + (4 if (c + 1) * X_CHUNK == BLOCKS else 0)):
                    k = j - c * X_CHUNK
                    if c + 1 < BLOCKS // X_CHUNK and k < 3:
                        chunk_deviation(c + 1, 2 * k)
                    if j == 1:
                        dve.wait_ge(w_hi, 1)
                        nc.vector.scalar_tensor_tensor(out=W16[:, 1, :, :], in0=w_sb, scalar=w_scale[:, 0:1],
                                                       in1=W16[:, 0, :, :], op0=ALU.mult, op1=ALU.subtract
                                                       ).then_inc(w_split, 1)
                        window_starts()
                    if j >= 2 and j - 2 < BLOCKS:
                        t = j - 2
                        dve.wait_ge(zT_hi, t + 1)
                        nc.vector.tensor_tensor(zT[:, t % 3, 1, :, :],
                                                bank[5 + t % 2][:, 0:DH * NB].rearrange("p (d n) -> p d n", d=DH),
                                                zT[:, t % 3, 0, :, :], ALU.subtract).then_inc(zT_ready, 1)
                    if j >= 4:
                        t = j - 4
                        dve.wait_ge(line_hi, t + 1)
                        nc.vector.tensor_tensor(line[:, t, 0:D], bank[t % 2][0:NB, 0:D], line[:, t, D:2 * D],
                                                ALU.subtract).then_inc(line_ready, 1)
                    if j + 2 * X_CHUNK < BLOCKS:
                        chunk_stats(j + 2 * X_CHUNK)
                    if c + 1 < BLOCKS // X_CHUNK and k < 3:
                        chunk_deviation(c + 1, 2 * k + 1)
                if (c + 3) * X_CHUNK <= BLOCKS:
                    chunk_to_root(c + 2)
                if c == 2:
                    window_edges()

            dve.wait_ge(edges_ps, 1)
            for t in range(WIN_TILES):
                nc.vector.tensor_tensor(rel[:, t, :], bank[2 + t][:, 0:NWP], row_thr[:, 0:NWP], ALU.subtract
                                        ).then_inc(dve_seq, 1)
                link(nc.vector.tensor_scalar(slot[:, t, :], bank[4 + t][:, 0:NWP], 1.0 / NB, -(NB - 1) / (2.0 * NB),
                                             ALU.mult, ALU.add))
                seq[0] += 1
            dve.wait_ge(dve_seq, seq[0])
            link(nc.vector.tensor_scalar(slot, slot, ROUND, None, ALU.add))
            link(nc.vector.tensor_scalar(slot, slot, ROUND, None, ALU.subtract))
            for t in range(WIN_TILES):
                link(nc.vector.scalar_tensor_tensor(out=part[:, t, :], in0=slot[:, t, :], scalar=-float(NB),
                                                    in1=bank[4 + t][:, 0:NWP], op0=ALU.mult, op1=ALU.add))
            link(nc.vector.scalar_tensor_tensor(out=key[:, :, :], in0=rel, scalar=float(BLOCKS), in1=slot,
                                                op0=ALU.mult, op1=ALU.add))
            nc.vector.memset(far_f[:, :], 0.0).then_inc(keys_ready, 1)
            dve.wait_ge(consts, 5)

            def finish(j, turn):
                if j == 0:
                    dve.wait_ge(b_in, 16)
                    dve.wait_ge(unscales_ready, 1)
                dve.wait_ge(sum_ps, turn + 1)
                number = ps_sum[turn % 2][0:NB, D:D + 1]
                nc.vector.tensor_scalar(has[:, :], number, 1.0, None, ALU.min).then_inc(linked[0], 1)
                seq[0] += 1
                link(nc.vector.tensor_scalar(inv[:, :], number, 1.0, None, ALU.max))
                link(nc.vector.reciprocal(inv[:, :], inv[:, :]))
                link(nc.vector.tensor_tensor(inv[:, :], inv[:, :], w_unscale[0:NB, 0:1], ALU.mult))
                link(nc.vector.scalar_tensor_tensor(out=x_sb[:, j, :], in0=b_bc[:, :], scalar=has[:, 0:1],
                                                    in1=x_sb[:, j, :], op0=ALU.mult, op1=ALU.add))
                nc.vector.scalar_tensor_tensor(out=x_sb[:, j, :], in0=ps_sum[turn % 2][0:NB, 0:D], scalar=inv[:, 0:1],
                                               in1=x_sb[:, j, :], op0=ALU.mult, op1=ALU.add).then_inc(x1_ready, 1)
                dve.wait_ge(x1_ready, turn + 1)
                norm_stats(j, x_sb[:, j, :])
                dve.wait_ge(linked[0], seq[0])
                to_root(j, j + 1)

            def second_norm(j, turn):
                inverse_deviation(j, j + 1)
                if turn >= 2:
                    dve.wait_ge(z2T_ps, turn - 1)
                nc.vector.tensor_scalar(z2[:, turn % 2, :], x_sb[:, j, :], mv[:, j, 0:1], rstd[:, j:j + 1],
                                        ALU.subtract, ALU.mult).then_inc(z2_ready, 1)

            def second_low(turn, buf, pos):
                dve.wait_ge(z2T_hi, turn + 1)
                nc.vector.tensor_tensor(z2T[:, buf, 1, :, pos, :],
                                        ps_zT[:, 0:DH * NB].rearrange("p (d n) -> p d n", d=DH),
                                        z2T[:, buf, 0, :, pos, :], ALU.subtract).then_inc(z2T_ready, 1)

            weights_work = {(0, 6): halve,
                            (0, 10): lambda: extreme(w_max, 1, flat(U_sb), ALU.max),
                            (1, 3): lambda: extreme(w_min, 1, flat(U_sb), ALU.min),
                            (1, 7): lambda: extreme(w_max, 2, flat(V_sb), ALU.max),
                            (1, 10): lambda: extreme(w_min, 2, flat(V_sb), ALU.min),
                            (2, 1): lambda: largest(1, 3),
                            (2, 10): lambda: scales(1, 3, 13, 2),
                            (3, 3): lambda: x_scales()}

            for j in range(BLOCKS + LAG):
                for i in range(WINDOWS):
                    w = j * WINDOWS + i
                    if j < BLOCKS:
                        if w >= HOTS:
                            dve.wait_ge(count_ps, w - HOTS + 1)
                        for t in range(WIN_TILES):
                            if not on_act(w):
                                nc.vector.tensor_scalar(hot_p[:, w % HOTS, t, :], iota[:, 0:P], part[:, t, w:w + 1],
                                                        None, ALU.is_equal).then_inc(dve_seq, 1)
                                seq[0] += 1
                            n = SPAN[w] * BLOCKS
                            ins = nc.vector.tensor_scalar(hot_ts[:, w % HOTS, t, 0:n], iota[:, 0:n],
                                                          key[:, t, w:w + 1], None, ALU.is_equal)
                        ins.then_inc(hot_ready, 1)
                    if (j, i) in weights_work:
                        weights_work[j, i]()
                    for at_i, behind in (FINISH_AT, NORM_AT, LOW_AT):
                        b = j - behind
                        early = (at_i, behind) == LOW_AT and (j, i) == (BLOCKS + 1, FINISH_AT[0] - 1)
                        b += early
                        if (i != at_i and not early) or not 0 <= b < BLOCKS or (b == BLOCKS - 2 and behind == LOW_AT[1]
                                                                              and not early):
                            continue
                        if (at_i, behind) == FINISH_AT:
                            finish(b, b)
                        elif (at_i, behind) == NORM_AT:
                            second_norm(b, b)
                        else:
                            second_low(b, b // TB % 2, b % TB)
                for n, (u, w, w16) in [(j - 4, of) for of in ((1, U_sb, U16), (2, V_sb, V16)) if 4 <= j < 7]:
                    dve.wait_ge(uv_hi, 2 * n + u)
                    nc.vector.scalar_tensor_tensor(out=w16[:, 1, :, n * H:(n + 1) * H], in0=w[:, :, n, :],
                                                   scalar=w_scale[:, u:u + 1], in1=w16[:, 0, :, n * H:(n + 1) * H],
                                                   op0=ALU.mult, op1=ALU.subtract).then_inc(uv_split, 1)
                if j == 6:
                    wide = limit.unsqueeze(1).to_broadcast([P, WIN_TILES, NWP])
                    link(nc.vector.tensor_scalar(inside, key[:, :, :], 0.0, None, ALU.is_ge))
                    link(nc.vector.tensor_tensor(rel, key[:, :, :], wide, ALU.is_lt))
                    link(nc.vector.tensor_tensor(inside, inside, rel, ALU.mult))
                    nc.vector.tensor_reduce(covered[:, :], inside.rearrange("p t w -> p (t w)"), AX_X, ALU.add
                                            ).then_inc(covered_ready, 1)
            dve.wait_ge(covered_ps, 1)
            link(nc.vector.tensor_scalar(open_f[:, :], ps_t[0][0:1, 0:1], float(E), None, ALU.not_equal))
            nc.vector.tensor_copy(open_i[:, :], open_f[:, :]).then_inc(open_ready, 1)

            chain = seq[0]
            linked[0], seq[0] = g_seq, 0

            def general_start():
                dve.wait_ge(g_in, 48)
                link(nc.vector.tensor_copy(g_dst_f, g_dst))

            def general_block(j):
                link(nc.vector.tensor_scalar(g_rel, g_dst_f, -float(j * NB), None, ALU.add))

                def one(e, b):
                    turn = e + j * EDGE_COLS
                    if not isinstance(e, int) or turn >= 2:
                        dve.wait_ge(g_used, turn - (0 if isinstance(e, int) and e == 0 else 1))
                        dve.sem_inc(waits_passed)
                    nc.vector.tensor_scalar(g_hot[:, b, :], iota[0:EDGE_ROWS, 0:P], g_rel[:, bass.ds(e, 1)], None,
                                            ALU.is_equal).then_inc(g_hot_ready, 1)
                tiles_of(dve, one)
                turn = BLOCKS + j
                finish(j, turn)
                second_norm(j, turn)
                second_low(turn, 0, 0)
                dve.wait_ge(gx_ready, MT * (len(BATCHES) + j + 1))

            where_open(dve, general_block, general_start)
            linked[0], seq[0] = dve_seq, chain

            dve.wait_ge(gx_ready, MT * len(BATCHES))
            nc.vector.memset(h_all[:, 0, :, 0:1], 0.0).then_inc(start_set, 1)
            nc.vector.memset(c_all[:, 0, :, 0:1], 0.0).then_inc(start_set, 1)
            dve.wait_ge(start_set, 2)

            def run_round(first, done, starts):
                if first == 0:
                    for q in range(2):
                        dve.wait_ge(h_ready[q], done + starts - 1)
                    dve.wait_ge(lo_ready[0], done + starts - 1)
                for q, (c0, c1) in enumerate(COLS):
                    if first == 0:
                        k0 = max(c0, 1)
                        nc.vector.tensor_copy(h_all[:, 0, :, k0:c1], h_all[:, STEPS, :, k0 - 1:c1 - 1]
                                              ).then_inc(h_ready[q], 1)
                    else:
                        nc.vector.memset(h_all[:, first, :, c0:c1], 0.0).then_inc(h_ready[q], 1)
                if first == 0:
                    nc.vector.tensor_copy(c_all[:, 0, :, 1:CHUNKS], c_all[:, STEPS, :, 0:CHUNKS - 1]
                                          ).then_inc(start_ready, 1)
                else:
                    nc.vector.memset(c_all[:, first, :, :], 0.0).then_inc(start_ready, 1)
                for q, (c0, c1) in enumerate(COLS):
                    dve.wait_ge(h_ready[q], done + starts)
                    nc.vector.tensor_scalar(h16[:, 0, :, c0:c1], h_all[:, first, :, c0:c1], 1.0, None, ALU.mult
                                            ).then_inc(hi_ready[q], 1)
                dve.wait_ge(start_ready, starts)
                dve.sem_inc(waits_passed)

                def step(q, s, turn):
                    c0, c1 = COLS[q]
                    n = c1 - c0
                    then = bass.ds(s + 1, 1)
                    def new_part():
                        dve.wait_ge(hc_ready[q], turn)
                        dve.wait_ge(ig_gate[q], turn)
                        nc.vector.scalar_tensor_tensor(out=ig[:, q, :, 0:n], in0=gate[:, q, 0:HH, 0:n], scalar=1.0,
                                                       in1=gate[:, q, HH:2 * HH, 0:n], op0=ALU.add, op1=ALU.mult
                                                       ).then_inc(ig_ready[q], 1)

                    def cell():
                        dve.wait_ge(ig_ready[q], turn)
                        nc.vector.scalar_tensor_tensor(out=c_all[:, then, :, c0:c1], in0=hc[:, q, :, 0:n], scalar=0.5,
                                                       in1=ig[:, q, :, 0:n], op0=ALU.mult, op1=ALU.add
                                                       ).then_inc(c_ready[q], 1)

                    def state():
                        dve.wait_ge(tc_ready[q], turn)
                        outs = [(h16[:, 0, :, c0:c1], hi_ready[q], 1), (h_all[:, then, :, c0:c1], h_ready[q], 1)]
                        if first > 0:
                            outs = outs[:1] if s < STEPS - 1 else [outs[0], (*outs[1][:2], STEPS - first)]
                        for to, ready, by in outs:
                            nc.vector.scalar_tensor_tensor(out=to, in0=gate[:, q, 2 * HH:MT, 0:n], scalar=1.0,
                                                           in1=tc[:, q, :, 0:n], op0=ALU.add, op1=ALU.mult
                                                           ).then_inc(ready, by)

                    new_part()
                    cell()
                    state()

                for q in range(2):
                    step(q, first, done + 1)
                for s in steps_of(dve, first, done):
                    for u in range(UNROLL):
                        for q in range(2):
                            step(q, s + u, s + (done - first + 1 + u))

            def count_near():
                for q in range(2):
                    dve.wait_ge(h_ready[q], DONE + len(ROUNDS))
                for n, state in enumerate((h_all, c_all)):
                    link(nc.vector.tensor_tensor(gap[:, n, :, :], state[:, STEPS, :, 0:CHUNKS - 1],
                                                 state[:, 0, :, 1:CHUNKS], ALU.subtract))
                link(nc.vector.tensor_tensor(gap[:, :, :, :], gap[:, :, :, :], gap[:, :, :, :], ALU.mult))
                link(nc.vector.tensor_scalar(gap[:, :, :, :], gap[:, :, :, :], STATE_TOL ** 2, None, ALU.is_le))
                nc.vector.tensor_reduce(near[:, :], gap[:, :, :, :].rearrange("p a m k -> p (a m k)"), AX_X, ALU.add
                                        ).then_inc(near_ready, 1)
                dve.wait_ge(near_ps, 1)
                link(nc.vector.tensor_scalar(far_f[:, :], ps_t[0][0:1, 0:1], float(P * 2 * HH * (CHUNKS - 1)), None,
                                             ALU.is_lt))
                nc.vector.tensor_copy(far_i[:, :], far_f[:, :]).then_inc(far_ready, 1)

            at_each_round(dve, run_round, count_near)

            for j in range(BLOCKS):
                dve.wait_ge(hT_ready, j + 1)
                nc.vector.scalar_tensor_tensor(out=x_sb[:, j, :], in0=ps_out[j % 4][0:NB, 0:H], scalar=0.5,
                                               in1=x_sb[:, j, :], op0=ALU.mult, op1=ALU.add).then_inc(out_ready, 1)


_INS = ['x', 'src', 'dst', 'L0_gnn_weight', 'L0_gnn_bias', 'L0_ffn_U_i', 'L0_ffn_V_i', 'L0_ffn_b_i',
        'L0_ffn_U_c', 'L0_ffn_V_c', 'L0_ffn_b_c', 'L0_ffn_U_o', 'L0_ffn_V_o', 'L0_ffn_b_o']


def kernel(**inputs):
    import numpy as _np
    import concourse.bacc as _bacc
    from concourse import mybir as _mybir
    from concourse.bass_utils import run_bass_kernel_spmd as _run

    nc = _bacc.Bacc("TRN2", target_bir_lowering=False, num_devices=1)
    arrays, args = {}, []
    for name in _INS:
        a = _np.ascontiguousarray(inputs[name])
        arrays[f"in_{name}_dram"] = a
        args.append(nc.dram_tensor(f"in_{name}_dram", a.shape, _mybir.dt.from_np(a.dtype), kind="ExternalInput").ap())
    args.append(nc.dram_tensor("out_0_dram", inputs["x"].shape, _mybir.dt.float32, kind="ExternalOutput").ap())
    bass_gnn_lstm_kernel(nc, *args)
    r = _run(nc, [arrays], core_ids=[0])
    return r.results[0]["out_0_dram"]
```
